# Optimizing a Trainium2 kernel written in Bass

```python
import numpy as np
import jax
import jax.numpy as jnp

def _softmax(x, axis=-1):
    return jax.nn.softmax(x, axis=axis)

def _gelu(x):
    return jax.nn.gelu(x, approximate=True)

def _silu(x):
    return jax.nn.silu(x)

def _sigmoid(x):
    return jax.nn.sigmoid(x)

def _layernorm(x, axis=-1, eps=1e-05):
    m = jnp.mean(x, axis=axis, keepdims=True)
    v = jnp.var(x, axis=axis, keepdims=True)
    return (x - m) / jnp.sqrt(v + eps)

def _scatter_add(tgt, idx, src, axis=0):
    return tgt.at[idx].add(src)

def _segment_sum(src, seg, n):
    return jax.ops.segment_sum(src, seg, n)
kernel_name = 'mk_seq_postln_d2_jaxref_r8_087658'

def setup_inputs(seed: int=0):
    np.random.seed(seed)
    _w = jnp.asarray

    def _L0_attn_setup():
        import jax, jax.numpy as jnp
        import numpy as np
        EMBED = 128
        HEADS = 16
        HEAD_DIM = EMBED // HEADS
        RANK = 8
        ALPHA = 16
        SCALING = ALPHA / RANK

        def _lora_linear(x, W, b, A, Bm):
            return x @ W + b + x @ A @ Bm * SCALING
        key = jax.random.key(seed)
        ks = jax.random.split(key, 9)
        s = 0.02
        x = jax.random.normal(ks[0], (4, 256, EMBED), dtype=jnp.float32)
        W_qkv = jax.random.normal(ks[1], (EMBED, 3 * EMBED), dtype=jnp.float32) * s
        b_qkv = jax.random.normal(ks[2], (3 * EMBED,), dtype=jnp.float32) * s
        A_qkv = jax.random.normal(ks[3], (EMBED, RANK), dtype=jnp.float32) * s
        B_qkv = jax.random.normal(ks[4], (RANK, 3 * EMBED), dtype=jnp.float32) * s
        W_proj = jax.random.normal(ks[5], (EMBED, EMBED), dtype=jnp.float32) * s
        b_proj = jax.random.normal(ks[6], (EMBED,), dtype=jnp.float32) * s
        A_proj = jax.random.normal(ks[7], (EMBED, RANK), dtype=jnp.float32) * s
        B_proj = jax.random.normal(ks[8], (RANK, EMBED), dtype=jnp.float32) * s
        return dict(x=x, W_qkv=W_qkv, b_qkv=b_qkv, A_qkv=A_qkv, B_qkv=B_qkv, W_proj=W_proj, b_proj=b_proj, A_proj=A_proj, B_proj=B_proj)
    _L0_attn_in = _L0_attn_setup()

    def _L0_ffn_setup():
        import jax, jax.numpy as jnp
        import numpy as np
        FP8_MAX = 448.0
        key = jax.random.key(seed)
        k_x, k_w, k_b = jax.random.split(key, 3)
        B, S, IN, OUT = (4, 1024, 128, 128)
        x = jax.random.normal(k_x, (B, S, IN), dtype=jnp.float32)
        w_fp32 = jax.random.normal(k_w, (OUT, IN), dtype=jnp.float32)
        weight_fp8 = w_fp32.astype(jnp.float8_e4m3fn).astype(jnp.float32)
        bias = jax.random.normal(k_b, (OUT,), dtype=jnp.float32)
        input_scale = jnp.ones((1,), dtype=jnp.float32)
        weight_scale = jnp.ones((1,), dtype=jnp.float32)
        return {'x': x, 'weight_fp8': weight_fp8, 'bias': bias, 'input_scale': input_scale, 'weight_scale': weight_scale}
    _L0_ffn_in = _L0_ffn_setup()

    def _L1_attn_setup():
        import jax, jax.numpy as jnp
        import numpy as np
        BATCH, SEQ = (2, 256)
        D_MODEL, D_STATE, D_CONV, EXPAND = (128, 16, 4, 2)
        D_INNER = EXPAND * D_MODEL

        def _selective_scan(xc, delta, A, Bm, Cm):
            dA = jnp.exp(delta[..., None] * A)
            dBx = delta[..., None] * Bm[:, :, None, :] * xc[..., None]
            h0 = jnp.zeros((xc.shape[0], xc.shape[2], A.shape[1]), xc.dtype)

            def step(h, inp):
                dA_t, dBx_t, c_t = inp
                h = dA_t * h + dBx_t
                y = jnp.einsum('bdn,bn->bd', h, c_t)
                return (h, y)
            _, ys = jax.lax.scan(step, h0, (dA.swapaxes(0, 1), dBx.swapaxes(0, 1), Cm.swapaxes(0, 1)))
            return ys.swapaxes(0, 1)

        def _forward(x, W_in, conv_w, conv_b, W_xproj, w_dt, b_dt, A_log, D_param, W_out):
            xz = x @ W_in
            x_inner, z = jnp.split(xz, 2, axis=-1)
            xc = jax.lax.conv_general_dilated(x_inner.swapaxes(1, 2), conv_w, window_strides=(1,), padding=[(D_CONV - 1, 0)], dimension_numbers=('NCH', 'OIH', 'NCH'), feature_group_count=D_INNER) + conv_b[None, :, None]
            xc = jax.nn.silu(xc.swapaxes(1, 2))
            x_ssm = xc @ W_xproj
            delta_raw = x_ssm[..., :1]
            Bm = x_ssm[..., 1:1 + D_STATE]
            Cm = x_ssm[..., 1 + D_STATE:]
            delta = jax.nn.softplus(delta_raw * w_dt + b_dt)
            A = -jnp.exp(A_log)
            y = _selective_scan(xc, delta, A, Bm, Cm)
            y = y + xc * D_param
            y = y * jax.nn.silu(z)
            return y @ W_out
        key = jax.random.key(seed)
        ks = jax.random.split(key, 8)
        x = jax.random.normal(ks[0], (BATCH, SEQ, D_MODEL), jnp.float32)
        W_in = jax.random.normal(ks[1], (D_MODEL, 2 * D_INNER), jnp.float32) * D_MODEL ** (-0.5)
        conv_w = jax.random.normal(ks[2], (D_INNER, 1, D_CONV), jnp.float32) * D_CONV ** (-0.5)
        conv_b = jnp.zeros((D_INNER,), jnp.float32)
        W_xproj = jax.random.normal(ks[3], (D_INNER, 2 * D_STATE + 1), jnp.float32) * D_INNER ** (-0.5)
        w_dt = jax.random.normal(ks[4], (D_INNER,), jnp.float32)
        b_dt = jnp.zeros((D_INNER,), jnp.float32)
        A_log = jnp.log(jnp.tile(jnp.arange(1, D_STATE + 1, dtype=jnp.float32), (D_INNER, 1)))
        D_param = jnp.ones((D_INNER,), jnp.float32)
        W_out = jax.random.normal(ks[5], (D_INNER, D_MODEL), jnp.float32) * D_INNER ** (-0.5)
        return dict(x=x, W_in=W_in, conv_w=conv_w, conv_b=conv_b, W_xproj=W_xproj, w_dt=w_dt, b_dt=b_dt, A_log=A_log, D_param=D_param, W_out=W_out)
    _L1_attn_in = _L1_attn_setup()

    def _L1_ffn_setup():
        import math
        import jax, jax.numpy as jnp
        import numpy as np
        NUM_EXPERTS = 8
        CAPACITY_FACTOR = 1.5
        key = jax.random.key(seed)
        ks = jax.random.split(key, 4)
        B, T, D, F, E = (4, 256, 128, 512, NUM_EXPERTS)
        scale = 0.02
        return {'x': jax.random.normal(ks[0], (B, T, D), dtype=jnp.float32), 'router_w': jax.random.normal(ks[1], (E, D), dtype=jnp.float32) * scale, 'w1': jax.random.normal(ks[2], (E, D, F), dtype=jnp.float32) * scale, 'b1': jnp.zeros((E, F), dtype=jnp.float32), 'w2': jax.random.normal(ks[3], (E, F, D), dtype=jnp.float32) * scale, 'b2': jnp.zeros((E, D), dtype=jnp.float32)}
    _L1_ffn_in = _L1_ffn_setup()
    _d = {'L0_attn_x': _L0_attn_in['x'], 'L0_attn_W_qkv': _L0_attn_in['W_qkv'], 'L0_attn_b_qkv': _L0_attn_in['b_qkv'], 'L0_attn_A_qkv': _L0_attn_in['A_qkv'], 'L0_attn_B_qkv': _L0_attn_in['B_qkv'], 'L0_attn_W_proj': _L0_attn_in['W_proj'], 'L0_attn_b_proj': _L0_attn_in['b_proj'], 'L0_attn_A_proj': _L0_attn_in['A_proj'], 'L0_attn_B_proj': _L0_attn_in['B_proj'], 'L0_ffn_weight_fp8': _L0_ffn_in['weight_fp8'], 'L0_ffn_bias': _L0_ffn_in['bias'], 'L0_ffn_input_scale': _L0_ffn_in['input_scale'], 'L0_ffn_weight_scale': _L0_ffn_in['weight_scale'], 'L1_attn_W_in': _L1_attn_in['W_in'], 'L1_attn_conv_w': _L1_attn_in['conv_w'], 'L1_attn_conv_b': _L1_attn_in['conv_b'], 'L1_attn_W_xproj': _L1_attn_in['W_xproj'], 'L1_attn_w_dt': _L1_attn_in['w_dt'], 'L1_attn_b_dt': _L1_attn_in['b_dt'], 'L1_attn_A_log': _L1_attn_in['A_log'], 'L1_attn_D_param': _L1_attn_in['D_param'], 'L1_attn_W_out': _L1_attn_in['W_out'], 'L1_ffn_router_w': _L1_ffn_in['router_w'], 'L1_ffn_w1': _L1_ffn_in['w1'], 'L1_ffn_b1': _L1_ffn_in['b1'], 'L1_ffn_w2': _L1_ffn_in['w2'], 'L1_ffn_b2': _L1_ffn_in['b2']}
    _x0 = _d['L0_attn_x']
    _d['L0_attn_x'] = jax.random.normal(jax.random.fold_in(jax.random.key(seed), 1), (8, 256, 128), dtype=_x0.dtype)
    del _x0
    return _d

def reference(L0_attn_x, L0_attn_W_qkv, L0_attn_b_qkv, L0_attn_A_qkv, L0_attn_B_qkv, L0_attn_W_proj, L0_attn_b_proj, L0_attn_A_proj, L0_attn_B_proj, L0_ffn_weight_fp8, L0_ffn_bias, L0_ffn_input_scale, L0_ffn_weight_scale, L1_attn_W_in, L1_attn_conv_w, L1_attn_conv_b, L1_attn_W_xproj, L1_attn_w_dt, L1_attn_b_dt, L1_attn_A_log, L1_attn_D_param, L1_attn_W_out, L1_ffn_router_w, L1_ffn_w1, L1_ffn_b1, L1_ffn_w2, L1_ffn_b2):

    def _L0_attn_ref(x, W_qkv, b_qkv, A_qkv, B_qkv, W_proj, b_proj, A_proj, B_proj):
        import jax, jax.numpy as jnp
        import numpy as np
        EMBED = 128
        HEADS = 16
        HEAD_DIM = EMBED // HEADS
        RANK = 8
        ALPHA = 16
        SCALING = ALPHA / RANK

        def _lora_linear(x, W, b, A, Bm):
            return x @ W + b + x @ A @ Bm * SCALING
        B, N, C = x.shape
        qkv = _lora_linear(x, W_qkv, b_qkv, A_qkv, B_qkv)
        qkv = qkv.reshape(B, N, 3, HEADS, HEAD_DIM).transpose(2, 0, 3, 1, 4)
        q, k, v = (qkv[0], qkv[1], qkv[2])
        attn = jnp.einsum('bhnd,bhmd->bhnm', q, k) * HEAD_DIM ** (-0.5)
        attn = jax.nn.softmax(attn, axis=-1)
        out = jnp.einsum('bhnm,bhmd->bhnd', attn, v)
        out = out.transpose(0, 2, 1, 3).reshape(B, N, C)
        return _lora_linear(out, W_proj, b_proj, A_proj, B_proj)

    def _L0_ffn_ref(x, weight_fp8, bias, input_scale, weight_scale):
        import jax, jax.numpy as jnp
        import numpy as np
        FP8_MAX = 448.0
        x_q = jnp.clip(x / input_scale, -FP8_MAX, FP8_MAX)
        x_dq = x_q.astype(jnp.float8_e4m3fn).astype(x.dtype) * input_scale
        w_dq = weight_fp8 * weight_scale
        out = jnp.einsum('bsi,oi->bso', x_dq, w_dq) + bias
        return out

    def _L1_attn_ref(x, W_in, conv_w, conv_b, W_xproj, w_dt, b_dt, A_log, D_param, W_out):
        import jax, jax.numpy as jnp
        import numpy as np
        BATCH, SEQ = (2, 256)
        D_MODEL, D_STATE, D_CONV, EXPAND = (128, 16, 4, 2)
        D_INNER = EXPAND * D_MODEL

        def _selective_scan(xc, delta, A, Bm, Cm):
            dA = jnp.exp(delta[..., None] * A)
            dBx = delta[..., None] * Bm[:, :, None, :] * xc[..., None]
            h0 = jnp.zeros((xc.shape[0], xc.shape[2], A.shape[1]), xc.dtype)

            def step(h, inp):
                dA_t, dBx_t, c_t = inp
                h = dA_t * h + dBx_t
                y = jnp.einsum('bdn,bn->bd', h, c_t)
                return (h, y)
            _, ys = jax.lax.scan(step, h0, (dA.swapaxes(0, 1), dBx.swapaxes(0, 1), Cm.swapaxes(0, 1)))
            return ys.swapaxes(0, 1)

        def _forward(x, W_in, conv_w, conv_b, W_xproj, w_dt, b_dt, A_log, D_param, W_out):
            xz = x @ W_in
            x_inner, z = jnp.split(xz, 2, axis=-1)
            xc = jax.lax.conv_general_dilated(x_inner.swapaxes(1, 2), conv_w, window_strides=(1,), padding=[(D_CONV - 1, 0)], dimension_numbers=('NCH', 'OIH', 'NCH'), feature_group_count=D_INNER) + conv_b[None, :, None]
            xc = jax.nn.silu(xc.swapaxes(1, 2))
            x_ssm = xc @ W_xproj
            delta_raw = x_ssm[..., :1]
            Bm = x_ssm[..., 1:1 + D_STATE]
            Cm = x_ssm[..., 1 + D_STATE:]
            delta = jax.nn.softplus(delta_raw * w_dt + b_dt)
            A = -jnp.exp(A_log)
            y = _selective_scan(xc, delta, A, Bm, Cm)
            y = y + xc * D_param
            y = y * jax.nn.silu(z)
            return y @ W_out
        return _forward(x, W_in, conv_w, conv_b, W_xproj, w_dt, b_dt, A_log, D_param, W_out)

    def _L1_ffn_ref(x, router_w, w1, b1, w2, b2):
        import math
        import jax, jax.numpy as jnp
        import numpy as np
        NUM_EXPERTS = 8
        CAPACITY_FACTOR = 1.5
        B, T, D = x.shape
        E = router_w.shape[0]
        N = B * T
        C = max(math.ceil(CAPACITY_FACTOR * N / E), 1)
        x_flat = x.reshape(N, D)
        logits = x_flat @ router_w.T
        probs = jax.nn.softmax(logits, axis=-1)
        chosen_e = jnp.argmax(probs, axis=-1)
        chosen_p = jnp.max(probs, axis=-1)
        onehot = jax.nn.one_hot(chosen_e, E, dtype=jnp.float32)
        pos = jnp.take_along_axis(jnp.cumsum(onehot, axis=0), chosen_e[:, None], axis=1)[:, 0] - 1.0
        pos = pos.astype(jnp.int32)
        kept = pos < C
        pos_c = jnp.clip(pos, 0, C - 1)
        buf = jnp.zeros((E, C, D), dtype=x.dtype).at[chosen_e, pos_c].add(x_flat * kept[:, None].astype(x.dtype))
        h = jax.nn.gelu(jnp.einsum('ecd,edf->ecf', buf, w1) + b1[:, None, :], approximate=False)
        eo = jnp.einsum('ecf,efd->ecd', h, w2) + b2[:, None, :]
        y = eo[chosen_e, pos_c] * (chosen_p * kept.astype(x.dtype))[:, None]
        return y.reshape(B, T, D)
    x = L0_attn_x
    x = _layernorm(x + _L0_attn_ref(x, L0_attn_W_qkv, L0_attn_b_qkv, L0_attn_A_qkv, L0_attn_B_qkv, L0_attn_W_proj, L0_attn_b_proj, L0_attn_A_proj, L0_attn_B_proj), axis=-1)
    x = _layernorm(x + _L0_ffn_ref(x, L0_ffn_weight_fp8, L0_ffn_bias, L0_ffn_input_scale, L0_ffn_weight_scale), axis=-1)
    x = _layernorm(x + _L1_attn_ref(x, L1_attn_W_in, L1_attn_conv_w, L1_attn_conv_b, L1_attn_W_xproj, L1_attn_w_dt, L1_attn_b_dt, L1_attn_A_log, L1_attn_D_param, L1_attn_W_out), axis=-1)
    x = _layernorm(x + _L1_ffn_ref(x, L1_ffn_router_w, L1_ffn_w1, L1_ffn_b1, L1_ffn_w2, L1_ffn_b2), axis=-1)
    return x

_drawn_inputs = setup_inputs


def setup_inputs(seed=0):
    import zlib

    import numpy as np

    out = dict(_drawn_inputs(seed))
    spreads = {'L1_attn_conv_b': (0.0, 0.1),
     'L1_attn_b_dt': (0.0, 0.342),
     'L1_attn_D_param': (1.0, 0.2),
     'L1_ffn_b1': (0.0, 0.8),
     'L1_ffn_b2': (0.0, 0.448)}
    factors = {'L0_attn_W_qkv': 4.025,
     'L0_attn_b_qkv': 3.384,
     'L0_attn_A_qkv': 8.0,
     'L0_attn_B_qkv': 8.0,
     'L0_attn_W_proj': 3.054,
     'L0_attn_A_proj': 7.385,
     'L0_attn_B_proj': 7.218,
     'L1_ffn_router_w': 2.922,
     'L1_ffn_w1': 6.105,
     'L1_ffn_w2': 5.499}
    for name, (base, spread) in spreads.items():
        noise = np.random.default_rng([zlib.crc32(name.encode()), seed]).standard_normal(out[name].shape)
        drawn = base * np.exp(spread * noise) if base else spread * noise
        out[name] = jnp.asarray(drawn.astype(out[name].dtype))
    for name, factor in factors.items():
        out[name] = (out[name] * factor).astype(out[name].dtype)
    return out
```

```python
from contextlib import ExitStack

import concourse.bass as bass
from concourse import mybir

F32 = mybir.dt.float32
BF16 = mybir.dt.bfloat16
I32 = mybir.dt.int32
U32 = mybir.dt.uint32
ALU = mybir.AluOpType
ACT = mybir.ActivationFunctionType
AX = mybir.AxisListType.X

P = 128
EPS = 1e-5
HEADS, HD = 16, 8
PAIRS = HEADS // 2
T = 512
TT = T // P
SEQ = 256
NB = T // SEQ
FP8_MAX = 448.0
STATES = 16
TAPS = 4
DB = 2
NC = 4
CHUNKS = STATES // NC
STEPS = CHUNKS * DB
EXPERTS = 8
FF = 512
FB = FF // P
QPARTS = (0, 1, 2, 0, 1, 0)
KPARTS = (0, 0, 0, 1, 1, 2)
LAG = 3
CONSTS = 14
CFRONT = 20
CBACK = 21
STACK = len(QPARTS) * HD


class Chain:

    def __init__(self, eng, sem, stage, per):
        self.eng, self.sem, self.base, self.per, self.n = eng, sem, stage * per, per, 0

    def link(self, ins):
        self.n += 1
        ins.then_inc(self.sem, 1)
        self.eng.wait_ge(self.sem, self.base + self.n)

    def done(self):
        assert self.n == self.per, (self.n, self.per)


def layers(nc, xT_in_d, x_in_d, wqkv_in, aqkvT_in, wproj_in, aprojT_in, rows_in, cols_in, wfp8T_in, scales_in,
           win_in, wx_in, wout_in, rwT_in, w1_in, b1c_in, w2_in, b2_in, buf, eo, parts, out):
    N = x_in_d.shape[0]
    GROUPS = N // T
    TILES = N // P
    CAP = -(-3 * N // (2 * EXPERTS))
    SLOTS = EXPERTS * CAP
    ST = CAP // P
    assert CAP % P == 0

    with ExitStack() as ctx:
        def sb(name, shape, dt=F32):
            return ctx.enter_context(nc.sbuf_tensor(name, shape, dt))

        def psum(name, shape=(P, 512), dt=F32):
            return ctx.enter_context(nc.psum_tensor(name, list(shape), dt))

        def sem(name):
            return ctx.enter_context(nc.semaphore(name))

        ident = sb("ident", [P, P])
        identb = sb("identb", [P, P], BF16)
        tri = sb("tri", [P, P])
        ones = sb("ones", [P, P])
        sel = sb("sel", [96, 2 * STATES, P], BF16)
        wqkv = sb("wqkv", [P, 384])
        wproj = sb("wproj", [P, P])
        aq = sb("aq", [8, P])
        bq = sb("bq", [8, 384])
        ap_ = sb("ap_", [8, P])
        bp = sb("bp", [8, P])
        rows = sb("rows", [P, 3 * P + 2 * P])
        cols = sb("cols", [P, 2 + DB * (TAPS + 3 + STATES)])
        wf = sb("wf", [P, P])
        scales = sb("scales", [P, 2])
        rscale = sb("rscale", [P, 1])
        win = sb("win", [P, 4 * P])
        wx = sb("wx", [P, DB, 33])
        wx96 = sb("wx96", [P, DB, 96])
        wd = sb("wd", [P, DB, DB * P])
        wout = sb("wout", [P, DB, P])
        rwT = sb("rwT", [P, EXPERTS])
        aneg = sb("aneg", [P, DB, STATES])
        key8 = sb("key8", [P, TT, EXPERTS])
        key8i = sb("key8i", [P, TT, EXPERTS], I32)
        dump = sb("dump", [P, TT])
        dumpi = sb("dumpi", [P, TT], I32)
        mhalf = sb("mhalf", [P, TT])
        carry = sb("carry", [P, EXPERTS])
        zeros = sb("zeros", [P, P])

        NCOL = 0

        def col(n):
            nonlocal NCOL
            a = cols[:, NCOL:NCOL + n]
            NCOL += n
            return a

        bqc, bkc = col(1), col(1)
        convw = col(DB * TAPS)
        convb, dpar, bdt = col(DB), col(DB), col(DB)
        alog = col(DB * STATES)
        bv_row = rows[:, 0:P]
        bproj_row = rows[:, P:2 * P]
        bff_row = rows[:, 2 * P:3 * P]
        wdt_row = rows[:, 3 * P:5 * P]

        xT = sb("xT", [P, T])
        xtok = sb("xtok", [P, TT, P])
        qf = sb("qf", [P, 2, T])
        qres = sb("qres", [P, 2, T])
        qparts = sb("qparts", [P, 2, 3, T], BF16)
        qs = sb("qs", [P, PAIRS, T], BF16)
        ks = sb("ks", [P, PAIRS, T], BF16)
        vaug = sb("vaug", [P, TT, HEADS, HD + 1])
        mx = sb("mx", [P, 8], BF16)
        mrow = sb("mrow", [8, P], BF16)
        probs = [sb(f"probs{n}", [P, 2, SEQ]) for n in range(4)]
        rden = sb("rden", [P, 8])
        otok = sb("otok", [P, TT, P])
        oT = sb("oT", [P, T])
        x1 = sb("x1", [P, TT, P])
        x1b = sb("x1b", [P, TT, P])
        x2 = sb("x2", [P, TT, P])
        res = sb("res", [P, TT, P])
        st6 = sb("st6", [P, TT, 6])
        mv = sb("mv", [P, TT, 2])
        vpe = sb("vpe", [P, TT])
        rstd = sb("rstd", [P, TT])
        qc = sb("qc", [P, T])
        qm = sb("qm", [P, T])
        xq = sb("xq", [P, T])
        x2T = sb("x2T", [P, T])
        xpad = sb("xpad", [P, DB, NB, SEQ + TAPS - 1])
        cacc = sb("cacc", [P, DB, T])
        xc = sb("xc", [P, DB, T])
        sz = sb("sz", [P, DB, T])
        pre = sb("pre", [P, DB, T])
        dlt = sb("dlt", [P, DB, T])
        dx = sb("dx", [P, DB, T])
        bct = sb("bct", [96, T], BF16)
        bcr = sb("bcr", [96, T])
        bcs = sb("bcs", [96, T], BF16)
        soft = sb("soft", [P, DB, T])
        brep = [sb(f"brep{n}", [P, NC, T]) for n in range(2)]
        crep = [sb(f"crep{n}", [P, NC, T]) for n in range(2)]
        da = [sb(f"da{n}", [P, NC, T]) for n in range(2)]
        u = [sb(f"u{n}", [P, NC, T]) for n in range(2)]
        yg = sb("yg", [P, DB, T])
        x3 = sb("x3", [P, TT, P])
        x3T = sb("x3T", [P, T])
        x3all = sb("x3all", [P, TILES, P])
        lg = sb("lg", [P, TT, EXPERTS])
        lge = sb("lge", [P, TT, EXPERTS])
        oh = sb("oh", [P, TT, EXPERTS])
        r4 = sb("r4", [P, 8, TT])
        sidx = sb("sidx", [P, TT], U32)
        gidx = sb("gidx", [P, TILES], U32)
        gate = sb("gate", [P, TILES])

        w1s = [da[0][:, n, :] for n in range(2)]
        w2s = [da[0][:, 2 + n, :].rearrange("p (f d) -> p f d", d=P) for n in range(2)]
        b2s = [da[1][:, 0, n * P:(n + 1) * P] for n in range(2)]
        xe = [da[1][:, 1 + n, 0:CAP].rearrange("p (t c) -> p t c", c=P) for n in range(2)]
        xeT = [da[1][:, 3, 0:CAP], u[0][:, 0, 0:CAP]]
        hT = [u[0][:, 1, 0:CAP], u[0][:, 2, 0:CAP], u[0][:, 3, 0:CAP], u[1][:, 0, 0:CAP]]
        ye = [u[1][:, 1 + n, 0:CAP].rearrange("p (t c) -> p t c", c=P) for n in range(2)]
        b1c = sb("b1c", [P, EXPERTS, FB])
        yall = brep[0][:].rearrange("p n t -> p (n t)").rearrange("p (t c) -> p t c", c=P)

        E = [psum("E0"), psum("E1")]
        M = psum("M")
        V = psum("V")
        GA = psum("GA")
        GM = psum("GM")
        Y = [psum("Y0"), psum("Y1")]

        w_in = sem("w_in")
        zeroed = sem("zeroed")
        consts = sem("consts")
        prep_pe, prep_act, prep_dve = sem("prep_pe"), sem("prep_act"), sem("prep_dve")
        xT_in, x_in = sem("xT_in"), sem("x_in")
        qkv_mm = sem("qkv_mm")
        parts_ready = sem("parts_ready")
        vaug_ready = sem("vaug_ready")
        parts_out = sem("parts_out")
        stack_in = sem("stack_in")
        max_mm, max_read = sem("max_mm"), sem("max_read")
        maxT_mm, mrow_ready = sem("maxT_mm"), sem("mrow_ready")
        mrow_in = sem("mrow_in")
        qk_mm, exp_done, pv_mm = sem("qk_mm"), sem("exp_done"), sem("pv_mm")
        norm_done = sem("norm_done")
        f_pe, f_act, f_dve, f_pool = sem("f_pe"), sem("f_act"), sem("f_dve"), sem("f_pool")
        FPE, FACT, FDVE, FPOOL = 9, 9, 6, 2
        var_ready, rstd_ready = sem("var_ready"), sem("rstd_ready")
        bc_mm, bc_read = sem("bc_mm"), sem("bc_read")
        da_ready = sem("da_ready")
        u_ready = sem("u_ready")
        h_ready = sem("h_ready")
        scanned = sem("scanned")
        y_mm = sem("y_mm")
        b_pe, b_act, b_dve = sem("b_pe"), sem("b_act"), sem("b_dve")
        BPE, BACT, BDVE = 4, 3, 5
        scattered = sem("scattered")
        c_att, c_front, c_back = sem("c_att"), sem("c_front"), sem("c_back")
        c_exp = sem("c_exp")
        b1_in = sem("b1_in")
        passed = sem("passed")
        we_in = [sem("we_in0"), sem("we_in1")]
        tok_in = [sem("tok_in0"), sem("tok_in1")]
        eo_out = [sem("eo_out0"), sem("eo_out1")]
        e_pe, e_act, e_dve = sem("e_pe"), sem("e_act"), sem("e_dve")
        EPE, EACT = 2 + FB, 1 + FB
        gathered = [sem(f"gathered{g}") for g in range(GROUPS)]
        z_dve = sem("z_dve")
        out_done = sem("out_done")

        block = ctx.enter_context(nc.Block())
        LOADS = 14
        PREP_DVE = 18

        def wait(eng, signal, count):
            if not isinstance(count, int) or count > 0:
                eng.wait_ge(signal, count)

        def wait_apart(eng, signal, count):
            wait(eng, signal, count)
            eng.sem_inc(passed, 1)

        def stages(eng, attend, front, beside, back):
            attend(0)
            front(0)
            with eng.Fori(0, GROUPS - 1) as g:
                beside(g, g + 1)
                back(g)
                front(g + 1)
            beside(GROUPS - 1, None)
            back(GROUPS - 1)

        def up_count(e, f):
            return 1 + EPE * e + f + 1

        def turn_count(e):
            return 1 if e == 0 else 1 + EPE * (e - 1) + FB + 1

        def down_count(e):
            return 1 + EPE * e + FB + (2 if e + 1 < EXPERTS else 1)

        @block.sync
        def _(sp):
            for dst, src in ((wqkv[:], wqkv_in), (wproj[:], wproj_in),
                             (aq[:], aqkvT_in[:, 0:P]), (bq[:], aqkvT_in[:, P:]),
                             (ap_[:], aprojT_in[:, 0:P]), (bp[:], aprojT_in[:, P:]),
                             (rows[:], rows_in.partition_broadcast(P)), (cols[:], cols_in),
                             (wf[:], wfp8T_in), (scales[:], scales_in.partition_broadcast(P)),
                             (win[:], win_in), (wx[:], wx_in.rearrange("(b p) n -> p b n", p=P)),
                             (wout[:], wout_in.rearrange("(b p) n -> p b n", p=P)), (rwT[:], rwT_in),
                             ):
                sp.dma_start(dst, src).then_inc(w_in, 16)
            sp.wait_ge(consts, CONSTS)
            for r in range(SLOTS // P):
                sp.dma_start(buf[r * P:(r + 1) * P, :], zeros[:]).then_inc(zeroed, 16)

            def attend(g):
                wait_apart(sp, qkv_mm, 3 * g)
                sp.dma_start(xT[:], xT_in_d[:, bass.ds(g * T, T)]).then_inc(xT_in, 16)
                wait_apart(sp, f_dve, FDVE * g)
                sp.dma_start(xtok[:], x_in_d[bass.ds(g * T, T), :].rearrange("(t p) c -> p t c", p=P)
                             ).then_inc(x_in, 16)
                sp.wait_ge(parts_ready, g + 1)
                for a, order in enumerate((QPARTS, KPARTS)):
                    for n, r in enumerate(order):
                        sp.dma_start(parts[a][:, n], qparts[:, a, r, :]).then_inc(parts_out, 16)
                wait_apart(sp, parts_out, 16 * 2 * len(QPARTS) * (g + 1))
                wait_apart(sp, pv_mm, 32 * g)
                for a, stack in enumerate((qs, ks)):
                    for i in range(2):
                        sp.dma_start(stack[64 * i:64 * i + STACK],
                                     parts[a].rearrange("(j i) n d t -> i (n d) j t", i=2)[i]
                                     ).then_inc(stack_in, 16)
                for q in range(8):
                    b, j = q // 4, 2 * (q % 4)
                    sp.wait_ge(mrow_ready, 8 * g + q + 1)
                    for i in range(2):
                        for jj in range(2):
                            dst = qs[64 * i + STACK:64 * i + STACK + 1, j + jj:j + jj + 1, b * SEQ:(b + 1) * SEQ]
                            sp.dma_start(dst.rearrange("o j (a t) -> o (j a) t", a=2),
                                         mrow[4 * i + 2 * jj:4 * i + 2 * jj + 2, :]).then_inc(mrow_in, 16)

            def beside(g, nxt):
                if nxt is not None:
                    attend(nxt)

            stages(sp, attend, lambda g: None, beside, lambda g: None)

            for e in range(EXPERTS):
                w = e % 2
                if e == 0:
                    sp.wait_ge(y_mm, 8 * GROUPS)
                if e >= 2:
                    sp.wait_ge(e_pe, down_count(e - 2))
                    sp.wait_ge(e_dve, e - 1)
                sp.dma_start(w1s[w], w1_in[e]).then_inc(we_in[w], 16)
                sp.dma_start(w2s[w], w2_in[e].rearrange("(f p) d -> p f d", p=P)).then_inc(we_in[w], 16)
                sp.dma_start(b2s[w], b2_in[e].partition_broadcast(P)).then_inc(we_in[w], 16)
                if e == 0:
                    sp.wait_ge(scattered, 16 * TILES)
                sp.dma_start(xe[w], buf[e * CAP:(e + 1) * CAP, :].rearrange("(t p) c -> p t c", p=P)
                             ).then_inc(tok_in[w], 16)
                if e >= 1:
                    sp.wait_ge(e_dve, e)
                    sp.dma_start(eo[(e - 1) * CAP:e * CAP, :].rearrange("(t p) c -> p t c", p=P), ye[1 - w]
                                 ).then_inc(eo_out[1 - w], 16)
            sp.wait_ge(e_dve, EXPERTS)
            sp.dma_start(eo[(EXPERTS - 1) * CAP:SLOTS, :].rearrange("(t p) c -> p t c", p=P),
                         ye[(EXPERTS - 1) % 2]).then_inc(eo_out[(EXPERTS - 1) % 2], 16)
            for g in range(GROUPS):
                sp.wait_ge(z_dve, g + 1)
                sp.dma_start(out[g * T:(g + 1) * T, :].rearrange("(t p) c -> p t c", p=P),
                             x3all[:, g * TT:(g + 1) * TT, :]).then_inc(out_done, 16)
            sp.wait_ge(out_done, 16 * GROUPS)

        @block.tensor
        def _(pe):
            pe.wait_ge(w_in, 16 * LOADS)
            pe.wait_ge(consts, CONSTS)
            pe.matmul(E[0][:, 0:384], aq[:], bq[:], start=True, stop=True)
            pe.matmul(E[1][:, 0:P], ap_[:], bp[:], start=True, stop=True).then_inc(prep_pe, 1)
            pe.wait_ge(prep_dve, PREP_DVE)

            def turn(dst, src, n=TT):
                for t in range(n):
                    last = pe.transpose(dst[:, t * P:(t + 1) * P], src[:, t, :], ident[:])
                return last

            def attend_pre(g):
                pe.wait_ge(xT_in, 16 * (g + 1))
                wait(pe, f_dve, FDVE * g)
                wait(pe, f_act, FACT * g)
                pe.matmul(E[0][:], wqkv[:, 0:P], xT[:], start=True, stop=True).then_inc(qkv_mm, 1)
                pe.matmul(E[1][:], wqkv[:, P:2 * P], xT[:], start=True, stop=True).then_inc(qkv_mm, 1)
                for t in range(TT):
                    last = pe.matmul(V[:, t * P:(t + 1) * P], xT[:, t * P:(t + 1) * P], wqkv[:, 2 * P:],
                                     start=True, stop=True)
                last.then_inc(qkv_mm, 1)

            def max_head(g, q, n):
                b, j, i = q // 4, 2 * (q % 4) + n // 2, n % 2
                if q == 0 and n == 0:
                    pe.wait_ge(stack_in, 64 * (g + 1))
                wait(pe, max_read, 32 * g + 4 * q + n)
                at = slice(64 * i, 64 * i + STACK)
                for t in range(2):
                    last = pe.matmul(M[:, t * SEQ:(t + 1) * SEQ],
                                     qs[at, j, b * SEQ + t * P:b * SEQ + (t + 1) * P],
                                     ks[at, j, b * SEQ:(b + 1) * SEQ], start=True, stop=True)
                last.then_inc(max_mm, 1)

            def max_turn(g, q):
                pe.wait_ge(max_read, 32 * g + 4 * q + 4)
                wait(pe, mrow_ready, 8 * g + q)
                pe.transpose(GA[0:8, 0:64].bitcast(BF16), mx[:], identb[:]).then_inc(maxT_mm, 1)

            def score_head(g, q, n):
                b, j, i = q // 4, 2 * (q % 4) + n // 2, n % 2
                h = 32 * g + 4 * q + n
                if n == 0:
                    pe.wait_ge(mrow_in, 64 * (8 * g + q + 1))
                if q == 0 and n < 2:
                    pe.wait_ge(parts_ready, g + 1)
                wait(pe, exp_done, h - 1)
                at = slice(64 * i, 64 * i + STACK + 1)
                for t in range(2):
                    last = pe.matmul(E[n % 2][:, t * SEQ:(t + 1) * SEQ],
                                     ks[at, j, b * SEQ + t * P:b * SEQ + (t + 1) * P],
                                     qs[at, j, b * SEQ:(b + 1) * SEQ], start=True, stop=True)
                last.then_inc(qk_mm, 1)

            def value_head(g, q, n):
                b, h = q // 4, 4 * (q % 4) + n
                pe.wait_ge(exp_done, 32 * g + 4 * q + n + 1)
                if n == 0:
                    if q == 0:
                        pe.wait_ge(vaug_ready, g + 1)
                    wait(pe, norm_done, 8 * g + q)
                for qt in range(2):
                    for kt in range(2):
                        c = (qt * 4 + n) * (HD + 1)
                        last = pe.matmul(V[:, c:c + HD + 1], probs[n][:, kt, qt * P:(qt + 1) * P],
                                         vaug[:, 2 * b + kt, h, :], start=(kt == 0), stop=(kt == 1))
                last.then_inc(pv_mm, 1)

            def spread(g, c):
                if c == 0:
                    pe.wait_ge(f_dve, FDVE * (g + 1))
                for k in range(2 * NC):
                    if c + k > 0:
                        pe.wait_ge(bc_read, 32 * g + 8 * c + k)
                    row = (k // NC) * STATES + NC * c + k % NC
                    pe.matmul(GM[:], sel[:, row, :], bcs[:], start=True, stop=True).then_inc(bc_mm, 1)

            def states_sum(g, st):
                c, db = st // DB, st % DB
                for half in range(2):
                    pe.wait_ge(h_ready, 2 * (8 * g + st) + half + 1)
                    for n in (2 * half, 2 * half + 1):
                        last = pe.matmul(Y[db][:], ident[:], u[st % 2][:, n, :], start=(c == 0 and n == 0),
                                         stop=(c == CHUNKS - 1 and n == NC - 1), skip_group_check=True)
                last.then_inc(y_mm, 1)

            def slots(g, nxt):
                if nxt is not None:
                    attend_pre(nxt)
                if g is not None:
                    spread(g, 0)
                for k in range(8 + LAG if nxt is not None else 8):
                    q = k - LAG
                    for n in range(4):
                        if nxt is not None and k < 8:
                            max_head(nxt, k, n)
                        if nxt is not None and q >= 0:
                            score_head(nxt, q, n)
                            if n > 0:
                                value_head(nxt, q, n - 1)
                    if g is not None and k < 8:
                        if k % 2 == 1 and k < 7:
                            spread(g, k // 2 + 1)
                        states_sum(g, k)
                    if nxt is not None and q >= 0:
                        value_head(nxt, q, 3)
                    if nxt is not None and k < 8:
                        max_turn(nxt, k)

            def front(g):
                at = FPE * g
                pe.wait_ge(norm_done, 8 * (g + 1))
                turn(E[0], otok).then_inc(f_pe, 1)
                pe.wait_ge(f_act, FACT * g + 1)
                for t in range(TT):
                    last = pe.matmul(E[1][:, t * P:(t + 1) * P], oT[:, t * P:(t + 1) * P], wproj[:],
                                     start=True, stop=True)
                last.then_inc(f_pe, 1)
                pe.wait_ge(f_dve, FDVE * g + 1)
                turn(M, x1).then_inc(f_pe, 1)
                pe.wait_ge(f_dve, FDVE * g + 2)
                for t in range(TT):
                    last = pe.matmul(V[:, t * P:(t + 1) * P], xq[:, t * P:(t + 1) * P], wf[:],
                                     start=True, stop=True)
                last.then_inc(f_pe, 1)
                pe.wait_ge(f_dve, FDVE * g + 3)
                turn(GA, x2).then_inc(f_pe, 1)
                pe.wait_ge(f_act, FACT * g + 2)
                for n, bank in enumerate((E[0], E[1], M, V)):
                    last = pe.matmul(bank[:], win[:, n * P:(n + 1) * P], x2T[:], start=True, stop=True)
                    if n % 2:
                        last.then_inc(f_pe, 1)
                pe.wait_ge(f_act, FACT * g + 7)
                for eb in range(DB):
                    last = pe.matmul(GA[0:96, :], wx96[:, eb, :], xc[:, eb, :], start=(eb == 0), stop=(eb == 1))
                last.then_inc(f_pe, 1)
                for db in range(DB):
                    for eb in range(DB):
                        last = pe.matmul(E[db][:], wd[:, eb, db * P:(db + 1) * P], xc[:, eb, :],
                                         start=(eb == 0), stop=(eb == 1))
                last.then_inc(f_pe, 1)

            def back(g):
                pe.wait_ge(b_dve, BDVE * g + 1)
                pe.wait_ge(bc_read, 32 * (g + 1))
                for t in range(TT):
                    for db in range(DB):
                        last = pe.matmul(GM[:, t * P:(t + 1) * P], yg[:, db, t * P:(t + 1) * P], wout[:, db, :],
                                         start=(db == 0), stop=(db == 1))
                last.then_inc(b_pe, 1)
                pe.wait_ge(b_dve, BDVE * g + 2)
                turn(GM, x3).then_inc(b_pe, 1)
                pe.wait_ge(b_act, BACT * g + 1)
                for t in range(TT):
                    last = pe.matmul(Y[0][:, t * 8:(t + 1) * 8], x3T[:, t * P:(t + 1) * P], rwT[:],
                                     start=True, stop=True)
                last.then_inc(b_pe, 1)
                pe.wait_ge(b_dve, BDVE * g + 4)
                for t in range(TT):
                    pe.matmul(Y[1][:, t * 8:(t + 1) * 8], tri[:], oh[:, t, :], start=True, stop=(t == 0))
                    for v in range(t):
                        pe.matmul(Y[1][:, t * 8:(t + 1) * 8], ones[:], oh[:, v, :], start=False, stop=(v == t - 1))
                for t in range(TT):
                    last = pe.matmul(Y[1][:, 32:40], ones[:], oh[:, t, :], start=(t == 0), stop=(t == TT - 1))
                last.then_inc(b_pe, 1)

            stages(pe, lambda g: slots(None, g), front, slots, back)

            def e_turn(e):
                pe.wait_ge(tok_in[e % 2], 16 * (e // 2 + 1))
                if e >= 2:
                    pe.wait_ge(e_act, EACT * (e - 2) + 1)
                turn((GA, GM)[e % 2], xe[e % 2], ST).then_inc(e_pe, 1)

            pe.wait_ge(b_dve, BDVE * GROUPS)
            e_turn(0)
            for e in range(EXPERTS):
                w = e % 2
                pe.wait_ge(we_in[w], 48 * (e // 2 + 1))
                pe.wait_ge(e_act, EACT * e + 1)
                for f, bank in enumerate((E[0], E[1], M, V)):
                    if e >= 1:
                        pe.wait_ge(e_act, EACT * (e - 1) + 2 + f)
                    pe.matmul(bank[:, 0:CAP], w1s[w][:, f * P:(f + 1) * P], xeT[w], start=True, stop=True
                              ).then_inc(e_pe, 1)
                if e + 1 < EXPERTS:
                    e_turn(e + 1)
                pe.wait_ge(e_act, EACT * e + 1 + FB)
                if e >= 2:
                    pe.wait_ge(e_dve, e - 1)
                for t in range(ST):
                    for f in range(FB):
                        last = pe.matmul(Y[w][:, t * P:(t + 1) * P], hT[f][:, t * P:(t + 1) * P], w2s[w][:, f, :],
                                         start=(f == 0), stop=(f == FB - 1))
                last.then_inc(e_pe, 1)

        @block.scalar
        def _(act):
            act.wait_ge(w_in, 16 * LOADS)
            act.activation(aneg[:].rearrange("p b n -> p (b n)"), alog, ACT.Exp).then_inc(prep_act, 1)
            act.dma_start(b1c[:], b1c_in).then_inc(b1_in, 16)
            act.wait_ge(b1_in, 16)
            act.wait_ge(consts, CONSTS)

            def exp_head(g, q, n):
                h = 32 * g + 4 * q + n
                act.wait_ge(qk_mm, h + 1)
                wait(act, pv_mm, h - 3)
                act.activation(probs[n][:].rearrange("p k t -> p (k t)"), E[n % 2][:], ACT.Exp).then_inc(exp_done, 1)

            def read_spread(g, c, ks_):
                if c >= 2:
                    act.wait_ge(u_ready, 2 * (8 * g + 2 * (c - 1)))
                    act.wait_ge(h_ready, 2 * (8 * g + 2 * (c - 1)))
                for k in ks_:
                    act.wait_ge(bc_mm, 32 * g + 8 * c + k + 1)
                    dst = (brep, crep)[k // NC][c % 2]
                    act.copy(dst[:, k % NC, :], GM[:]).then_inc(bc_read, 1)

            def decay(g, st):
                c, db = st // DB, st % DB
                if st == 0:
                    act.wait_ge(f_dve, FDVE * (g + 1))
                    act.wait_ge(prep_dve, PREP_DVE)
                if st >= 2:
                    act.wait_ge(scanned, 2 * (8 * g + st - 1))
                for n in range(NC):
                    last = act.activation(da[st % 2][:, n, :], dlt[:, db, :], ACT.Exp,
                                          scale=aneg[:, db, NC * c + n:NC * c + n + 1])
                last.then_inc(da_ready, 1)

            def slots(g, nxt):
                if g is not None:
                    decay(g, 0)
                    read_spread(g, 0, range(2 * NC))
                for k in range(8 + LAG if nxt is not None else 8):
                    q = k - LAG
                    for n in range(4):
                        if nxt is not None and q >= 0:
                            exp_head(nxt, q, n)
                    if g is not None and k < 7:
                        decay(g, k + 1)
                        if k % 2 == 1:
                            read_spread(g, k // 2 + 1, range(2 * NC))

            def front(g):
                act.wait_ge(f_pe, FPE * g + 1)
                act.copy(oT[:], E[0][:]).then_inc(f_act, 1)
                act.wait_ge(f_pe, FPE * g + 5)
                act.copy(x2T[:], GA[:]).then_inc(f_act, 1)
                act.wait_ge(f_pe, FPE * g + 6)
                for db in range(DB):
                    act.copy(xpad[:, db, :, TAPS - 1:], E[db][:].rearrange("p (b t) -> p b t", b=NB)
                             ).then_inc(f_act, 1)
                act.wait_ge(f_pe, FPE * g + 7)
                for db, bank in enumerate((M, V)):
                    act.activation(sz[:, db, :], bank[:], ACT.Silu).then_inc(f_act, 1)
                act.wait_ge(f_dve, FDVE * g + 4)
                act.activation(xc[:], cacc[:], ACT.Silu).then_inc(f_act, 1)
                act.wait_ge(f_dve, FDVE * g + 5)
                act.activation(soft[:], cacc[:], ACT.Exp).then_inc(f_act, 1)
                act.wait_ge(f_act, FACT * g + 8)
                act.activation(soft[:], soft[:], ACT.Ln, bias=1.0).then_inc(f_act, 1)

            def back(g):
                act.wait_ge(b_pe, BPE * g + 2)
                act.copy(x3T[:], GM[:]).then_inc(b_act, 1)
                act.wait_ge(b_dve, BDVE * g + 3)
                act.activation(lge[:], lg[:], ACT.Exp).then_inc(b_act, 1)
                act.copy(x3all[:, bass.ds(g * TT, TT), :], x3[:]).then_inc(b_act, 1)

            stages(act, lambda g: slots(None, g), front, slots, back)

            for e in range(EXPERTS):
                act.wait_ge(e_pe, turn_count(e))
                act.copy(xeT[e % 2], (GA, GM)[e % 2][:, 0:CAP]).then_inc(e_act, 1)
                for f, bank in enumerate((E[0], E[1], M, V)):
                    act.wait_ge(e_pe, up_count(e, f))
                    if e >= 1 and f == 0:
                        act.wait_ge(e_pe, down_count(e - 1))
                    act.activation(hT[f], bank[:, 0:CAP], ACT.Gelu, bias=b1c[:, e, f:f + 1]).then_inc(e_act, 1)

        @block.vector
        def _(dve):
            prep = Chain(dve, prep_dve, 0, PREP_DVE)
            dve.wait_ge(w_in, 16 * LOADS)
            dve.wait_ge(consts, CONSTS)
            dve.wait_ge(prep_act, 1)
            prep.link(dve.tensor_scalar(aneg[:], aneg[:], -1.0, None, ALU.mult))
            for eb in range(DB):
                for r in range(3):
                    prep.link(dve.tensor_copy(wx96[:, eb, 32 * r:32 * (r + 1)], wx[:, eb, 1:33]))
                prep.link(dve.tensor_scalar(wd[:, eb, :], wdt_row, wx[:, eb, 0:1], None, ALU.mult))
            prep.link(dve.tensor_scalar(wf[:], wf[:], scales[:, 0:1], scales[:, 1:2], ALU.mult, ALU.mult))
            prep.link(dve.reciprocal(rscale[:], scales[:, 0:1]))
            prep.link(dve.tensor_copy(key8[:], key8i[:]))
            prep.link(dve.tensor_copy(dump[:], dumpi[:]))
            prep.link(dve.memset(ks[:], 1.0))
            dve.wait_ge(prep_pe, 1)
            prep.link(dve.scalar_tensor_tensor(wqkv[:], E[0][:, 0:384], 2.0, wqkv[:], ALU.mult, ALU.add))
            prep.link(dve.scalar_tensor_tensor(wproj[:], E[1][:, 0:P], 2.0, wproj[:], ALU.mult, ALU.add))
            prep.link(dve.memset(carry[:], 0.0))
            prep.link(dve.memset(xpad[:], 0.0))
            prep.done()

            def norm(ch, count, dst):
                for t in range(TT):
                    last = dve.bn_stats(st6[:, t, :], res[:, t, :])
                ch.n += 1
                last.then_inc(ch.sem, 1)
                wait_apart(dve, ch.sem, ch.base + ch.n)
                for t in range(TT):
                    last = dve.bn_aggr(mv[:, t, :], st6[:, t, :])
                ch.link(last)
                dve.tensor_scalar(vpe[:], mv[:, :, 1], EPS, None, ALU.add).then_inc(var_ready, 1)
                dve.wait_ge(rstd_ready, count)
                for t in range(TT):
                    last = dve.tensor_scalar(dst[:, t, :], res[:, t, :], mv[:, t, 0:1], rstd[:, t:t + 1],
                                             ALU.subtract, ALU.mult)
                return last

            def attend_pre(g):
                ch = Chain(dve, c_att, g, 5)
                wait(dve, parts_out, 16 * 2 * len(QPARTS) * g)
                dve.wait_ge(qkv_mm, 3 * g + 1)
                dve.tensor_scalar(qf[:, 0, :], E[0][:], bqc, HD ** -0.5, ALU.add, ALU.mult)
                dve.wait_ge(qkv_mm, 3 * g + 2)
                ch.link(dve.tensor_scalar(qf[:, 1, :], E[1][:], bkc, None, ALU.add))
                ch.link(dve.tensor_copy(qparts[:, :, 0, :], qf[:]))
                ch.link(dve.tensor_tensor(qres[:], qf[:], qparts[:, :, 0, :], ALU.subtract))
                ch.link(dve.tensor_copy(qparts[:, :, 1, :], qres[:]))
                dve.tensor_tensor(qparts[:, :, 2, :], qres[:], qparts[:, :, 1, :], ALU.subtract
                                  ).then_inc(parts_ready, 1)
                dve.wait_ge(qkv_mm, 3 * g + 3)
                ch.link(dve.memset(vaug[:, :, :, HD:], 1.0))
                dve.tensor_tensor(vaug[:, :, :, 0:HD].rearrange("p t h d -> p t (h d)") if False else
                                  vaug[:, :, :, 0:HD], V[:].rearrange("p (t h d) -> p t h d", t=TT, d=HD),
                                  bv_row.rearrange("p (h d) -> p h d", d=HD).unsqueeze(1)
                                  .to_broadcast([P, TT, HEADS, HD]), ALU.add).then_inc(vaug_ready, 1)
                ch.done()

            def head_max(g, q, n):
                dve.wait_ge(max_mm, 32 * g + 4 * q + n + 1)
                if n == 0:
                    wait(dve, maxT_mm, 8 * g + q)
                c = 4 * (n % 2) + 2 * (n // 2)
                dve.tensor_reduce(mx[:, c:c + 2], M[:].rearrange("p (t k) -> p t k", t=2), AX, ALU.max
                                  ).then_inc(max_read, 1)

            def max_rows(g, q):
                dve.wait_ge(maxT_mm, 8 * g + q + 1)
                wait(dve, mrow_in, 64 * (8 * g + q))
                dve.tensor_scalar(mrow[:], GA[0:8, 0:64].bitcast(BF16), -1.0, None, ALU.mult
                                  ).then_inc(mrow_ready, 1)

            def divide(g, q):
                b = q // 4
                ch = Chain(dve, c_exp, 8 * g + q, 1)
                dve.wait_ge(pv_mm, 32 * g + 4 * q + 4)
                v = V[:, 0:8 * (HD + 1)].rearrange("p (t n d) -> p t n d", t=2, n=4)
                ch.link(dve.reciprocal(rden[:], v[:, :, :, HD].rearrange("p t n -> p t n")))
                h = 4 * (q % 4)
                dve.tensor_tensor(otok[:, 2 * b:2 * b + 2, h * HD:(h + 4) * HD].rearrange("p t (n d) -> p t n d", d=HD),
                                  v[:, :, :, 0:HD],
                                  rden[:].rearrange("p (t n) -> p t n", t=2).unsqueeze(3).to_broadcast([P, 2, 4, HD]),
                                  ALU.mult).then_inc(norm_done, 1)
                ch.done()

            def scan_half(g, st, half):
                c, at = st // DB, slice(2 * half, 2 * half + 2)
                if half == 0:
                    dve.wait_ge(u_ready, 2 * (8 * g + st + 1))
                ub = u[st % 2][:, at, :].rearrange("p n t -> p (n t)")
                dve.tensor_tensor_scan(ub, da[st % 2][:, at, :].rearrange("p n t -> p (n t)"), ub, 0.0,
                                       ALU.mult, ALU.add).then_inc(scanned, 1)

            def gate_half(g, st, half):
                c, at = st // DB, slice(2 * half, 2 * half + 2)
                dve.wait_ge(scanned, 2 * (8 * g + st) + half + 1)
                dve.wait_ge(bc_read, 32 * g + 8 * c + 8)
                dve.tensor_tensor(u[st % 2][:, at, :], u[st % 2][:, at, :], crep[c % 2][:, at, :], ALU.mult
                                  ).then_inc(h_ready, 1)

            def slots(g, nxt):
                if nxt is not None:
                    attend_pre(nxt)
                for k in range(8 + LAG if nxt is not None else 8):
                    q = k - LAG
                    for n in range(4):
                        if nxt is not None and k < 8:
                            head_max(nxt, k, n)
                        if g is not None and k < 8:
                            (scan_half, gate_half)[n % 2](g, k, n // 2)
                    if nxt is not None and k < 8:
                        max_rows(nxt, k)
                    if nxt is not None and q >= 0:
                        divide(nxt, q)

            def front(g):
                ch = Chain(dve, c_front, g, CFRONT)
                flat = lambda a: a.rearrange("p t c -> p (t c)")
                dve.wait_ge(f_pe, FPE * g + 2)
                dve.wait_ge(f_pool, FPOOL * g + 1)
                ch.link(dve.tensor_tensor(flat(res[:]), E[1][:], flat(xtok[:]), ALU.add))
                norm(ch, 3 * g + 1, x1).then_inc(f_dve, 1)
                dve.wait_ge(f_pe, FPE * g + 3)
                ch.link(dve.tensor_scalar(qc[:], M[:], rscale[:, 0:1], FP8_MAX, ALU.mult, ALU.min))
                ch.link(dve.tensor_scalar(qc[:], qc[:], -FP8_MAX, None, ALU.max))
                ch.link(dve.tensor_scalar(qm[:].bitcast(I32), qc[:].bitcast(I32), 0x7F800000, None, ALU.bitwise_and))
                ch.link(dve.tensor_scalar(qm[:], qm[:], 2.0 ** -6, 1.5 * 2.0 ** 20, ALU.max, ALU.mult))
                ch.link(dve.tensor_tensor(qc[:], qc[:], qm[:], ALU.add))
                dve.tensor_tensor(xq[:], qc[:], qm[:], ALU.subtract).then_inc(f_dve, 1)
                dve.wait_ge(f_pe, FPE * g + 4)
                dve.wait_ge(f_pool, FPOOL * g + 2)
                ch.link(dve.tensor_tensor(flat(res[:]), V[:], flat(x1b[:]), ALU.add))
                norm(ch, 3 * g + 2, x2).then_inc(f_dve, 1)
                dve.wait_ge(f_act, FACT * g + 4)
                for k in range(TAPS):
                    for db in range(DB):
                        src = xpad[:, db, :, k:k + SEQ]
                        dst = cacc[:, db, :].rearrange("p (b t) -> p b t", b=NB)
                        w = convw[:, db * TAPS + k:db * TAPS + k + 1]
                        if k == 0:
                            last = dve.tensor_scalar(dst, src, w, convb[:, db:db + 1], ALU.mult, ALU.add)
                        else:
                            last = dve.scalar_tensor_tensor(dst, src, w, dst, ALU.mult, ALU.add)
                    if k < TAPS - 1:
                        ch.link(last)
                last.then_inc(f_dve, 1)
                dve.wait_ge(f_pe, FPE * g + 8)
                ch.link(dve.tensor_copy(bct[:], GA[0:96, :]))
                ch.link(dve.tensor_tensor(bcr[:], GA[0:96, :], bct[:], ALU.subtract))
                ch.link(dve.tensor_copy(bcs[:], bcr[:]))
                dve.tensor_copy(bcs[0:32, :], bct[0:32, :])
                ch.link(dve.tensor_tensor(bcs[64:96, :], bcr[64:96, :], bcs[64:96, :], ALU.subtract))
                dve.wait_ge(f_pe, FPE * g + 9)
                dve.tensor_scalar(pre[:, 0, :], E[0][:], bdt[:, 0:1], None, ALU.add)
                ch.link(dve.tensor_scalar(pre[:, 1, :], E[1][:], bdt[:, 1:2], None, ALU.add))
                dve.scalar_tensor_tensor(cacc[:], pre[:], -1.0, pre[:], ALU.mult, ALU.min).then_inc(f_dve, 1)
                dve.wait_ge(f_act, FACT * g + 9)
                ch.link(dve.scalar_tensor_tensor(dlt[:], pre[:], 0.0, soft[:], ALU.max, ALU.add))
                dve.tensor_tensor(dx[:], dlt[:], xc[:], ALU.mult).then_inc(f_dve, 1)
                ch.done()

            def back(g):
                ch = Chain(dve, c_back, g, CBACK)
                dve.wait_ge(y_mm, 8 * (g + 1))
                for db in range(DB):
                    last = dve.scalar_tensor_tensor(yg[:, db, :], xc[:, db, :], dpar[:, db:db + 1], Y[db][:],
                                                    ALU.mult, ALU.add)
                ch.link(last)
                dve.tensor_tensor(yg[:], yg[:], sz[:], ALU.mult).then_inc(b_dve, 1)
                dve.wait_ge(b_pe, BPE * g + 1)
                ch.link(dve.tensor_tensor(res[:].rearrange("p t c -> p (t c)"), GM[:],
                                          x2[:].rearrange("p t c -> p (t c)"), ALU.add))
                norm(ch, 3 * g + 3, x3).then_inc(b_dve, 1)
                top, total, prob, kmax, pos, first, kept, slot = (r4[:, n, :] for n in range(8))
                wide = lambda a: a.unsqueeze(2).to_broadcast([P, TT, EXPERTS])
                dve.wait_ge(b_pe, BPE * g + 3)
                ch.link(dve.tensor_copy(lg[:].rearrange("p t e -> p (t e)"), Y[0][:, 0:TT * EXPERTS]))
                ch.link(dve.tensor_reduce(top, lg[:], AX, ALU.max))
                dve.tensor_tensor(lg[:], lg[:], wide(top), ALU.subtract).then_inc(b_dve, 1)
                dve.wait_ge(b_dve, BDVE * g + 3)
                ch.link(dve.scalar_tensor_tensor(oh[:], lg[:], 0.0, key8[:], ALU.is_ge, ALU.mult))
                ch.link(dve.tensor_reduce(kmax, oh[:], AX, ALU.max))
                dve.tensor_tensor(oh[:], key8[:], wide(kmax), ALU.is_equal).then_inc(b_dve, 1)
                dve.wait_ge(b_act, BACT * g + 2)
                ch.link(dve.tensor_reduce(total, lge[:], AX, ALU.add))
                ch.link(dve.reciprocal(prob, total))
                dve.tensor_scalar(first, kmax, -float(CAP), float(CAP * EXPERTS), ALU.mult, ALU.add)
                dve.wait_ge(b_pe, BPE * g + 4)
                ch.link(dve.tensor_tensor(lge[:], Y[1][:, 0:TT * EXPERTS].rearrange("p (t e) -> p t e", t=TT),
                                          carry[:].unsqueeze(1).to_broadcast([P, TT, EXPERTS]), ALU.add))
                ch.link(dve.tensor_tensor(lge[:], lge[:], oh[:], ALU.mult))
                dve.tensor_tensor(carry[:], carry[:], Y[1][:, 32:32 + EXPERTS], ALU.add)
                ch.link(dve.tensor_reduce(pos, lge[:], AX, ALU.add))
                ch.link(dve.tensor_scalar(kept, pos, float(CAP), None, ALU.is_le))
                ch.link(dve.tensor_tensor(gate[:, bass.ds(g * TT, TT)], prob, kept, ALU.mult))
                ch.link(dve.tensor_scalar(slot, pos, float(CAP), -1.0, ALU.min, ALU.add))
                ch.link(dve.tensor_tensor(slot, slot, first, ALU.add))
                dve.tensor_copy(gidx[:, bass.ds(g * TT, TT)], slot)
                ch.link(dve.tensor_tensor(pos, slot, dump[:], ALU.subtract))
                ch.link(dve.tensor_tensor(pos, pos, kept, ALU.mult))
                ch.link(dve.tensor_tensor(pos, pos, dump[:], ALU.add))
                ch.link(dve.tensor_scalar(dump[:], dump[:], float(T), None, ALU.add))
                dve.tensor_copy(sidx[:], pos).then_inc(b_dve, 1)
                ch.done()

            stages(dve, lambda g: slots(None, g), front, slots, back)

            for e in range(EXPERTS):
                w = e % 2
                dve.wait_ge(we_in[w], 48 * (e // 2 + 1))
                dve.wait_ge(e_pe, down_count(e))
                if e >= 2:
                    dve.wait_ge(eo_out[w], 16 * (e // 2))
                dve.tensor_tensor(ye[w], Y[w][:, 0:CAP].rearrange("p (t c) -> p t c", c=P),
                                  b2s[w].unsqueeze(1).to_broadcast([P, ST, P]), ALU.add).then_inc(e_dve, 1)
            for g in range(GROUPS):
                ch = Chain(dve, c_back, 0, CBACK * GROUPS + 4 * (g + 1))
                ch.n = CBACK * GROUPS + 4 * g
                mine = x3all[:, g * TT:(g + 1) * TT, :]
                got = yall[:, g * TT:(g + 1) * TT, :]
                dve.wait_ge(gathered[g], 16 * TT)
                dve.wait_ge(b_act, BACT * GROUPS)
                ch.link(dve.tensor_tensor(got, got, gate[:, g * TT:(g + 1) * TT].unsqueeze(2)
                                          .to_broadcast([P, TT, P]), ALU.mult))
                ch.link(dve.tensor_tensor(res[:], got, mine, ALU.add))
                norm(ch, 3 * GROUPS + g + 1, mine).then_inc(z_dve, 1)
                ch.done()

        @block.gpsimd
        def _(pool):
            pool.memset(zeros[:], 0.0).then_inc(consts, 1)
            pool.memset(ident[:], 0.0).then_inc(consts, 1)
            pool.memset(identb[:], 0.0).then_inc(consts, 1)
            pool.memset(ones[:], 1.0).then_inc(consts, 1)
            pool.memset(sel[:], 0.0).then_inc(consts, 1)
            pool.memset(mhalf[:], -0.5).then_inc(consts, 1)
            pool.iota(key8i[:], pattern=[[0, TT], [-1, EXPERTS]], base=EXPERTS, channel_multiplier=0
                      ).then_inc(consts, 1)
            pool.iota(dumpi[:], pattern=[[P, TT]], base=SLOTS, channel_multiplier=1).then_inc(consts, 1)
            pool.wait_ge(consts, 8)
            for m in (ident, identb):
                pool.affine_select(out=m[:], in_=m[:], compare_op=ALU.not_equal, fill=1.0, base=0,
                                   pattern=[[-1, P]], channel_multiplier=1).then_inc(consts, 1)
            pool.affine_select(out=tri[:], in_=ones[:], compare_op=ALU.is_ge, fill=0.0, base=0,
                               pattern=[[1, P]], channel_multiplier=-1).then_inc(consts, 1)
            for r in range(3):
                pool.affine_select(out=sel[:], in_=sel[:], compare_op=ALU.not_equal, fill=1.0, base=-32 * r,
                                   pattern=[[-1, 2 * STATES], [0, P]], channel_multiplier=1).then_inc(consts, 1)
                pool.wait_ge(consts, 12 + r)
            assert CONSTS == 14

            def power(count):
                pool.wait_ge(var_ready, count)
                pool.tensor_tensor(rstd[:], vpe[:], mhalf[:], ALU.pow).then_inc(rstd_ready, 1)

            def increments(g, st):
                c, db = st // DB, st % DB
                if st == 0:
                    pool.wait_ge(f_dve, FDVE * (g + 1))
                pool.wait_ge(bc_read, 32 * g + 8 * c + 4)
                if st >= 2:
                    pool.wait_ge(y_mm, 8 * g + st - 1)
                pool.tensor_tensor(u[st % 2][:], brep[c % 2][:],
                                   dx[:, db, :].unsqueeze(1).to_broadcast([P, NC, T]), ALU.mult).then_inc(u_ready, 1)
                wait_apart(pool, da_ready, 8 * g + st + 1)
                pool.memset(da[st % 2][:].rearrange("p n (b t) -> p n b t", b=NB)[:, :, :, 0:1], 0.0
                            ).then_inc(u_ready, 1)

            def beside(g, nxt):
                for st in range(8):
                    increments(g, st)

            def front(g):
                pool.wait_ge(x_in, 16 * (g + 1))
                pool.wait_ge(w_in, 16 * LOADS)
                pool.tensor_tensor(xtok[:], xtok[:], bproj_row.unsqueeze(1).to_broadcast([P, TT, P]), ALU.add
                                   ).then_inc(f_pool, 1)
                power(3 * g + 1)
                pool.wait_ge(f_dve, FDVE * g + 1)
                pool.tensor_tensor(x1b[:], x1[:], bff_row.unsqueeze(1).to_broadcast([P, TT, P]), ALU.add
                                   ).then_inc(f_pool, 1)
                power(3 * g + 2)

            def back(g):
                power(3 * g + 3)
                wait_apart(pool, b_dve, BDVE * (g + 1))
                pool.wait_ge(zeroed, 16 * (SLOTS // P))
                for t in range(TT):
                    pool.indirect_dma_start(buf, bass.IndirectOffsetOnAxis(ap=sidx[:, t:t + 1], axis=0),
                                            x3[:, t, :], None).then_inc(scattered, 16)
                pool.wait_ge(scattered, 16 * TT * (g + 1))

            stages(pool, lambda g: None, front, beside, back)

            pool.wait_ge(eo_out[0], 16 * (EXPERTS // 2))
            pool.wait_ge(eo_out[1], 16 * (EXPERTS // 2))
            for t in range(TILES):
                pool.indirect_dma_start(yall[:, t, :], None, eo,
                                        bass.IndirectOffsetOnAxis(ap=gidx[:, t:t + 1], axis=0)
                                        ).then_inc(gathered[t // TT], 16)
            for g in range(GROUPS):
                power(3 * GROUPS + g + 1)


def kernel(**inputs):
    import numpy as np
    import concourse.bacc as bacc
    from concourse.bass_utils import run_bass_kernel_spmd as run

    a = {k: np.asarray(v) for k, v in inputs.items()}
    x = a["L0_attn_x"]
    B, S, C = x.shape
    flat = x.reshape(B * S, C)
    by_block = lambda v: v.reshape(DB, P, -1).transpose(1, 0, 2).reshape(P, -1)
    bq = a["L0_attn_b_qkv"]
    arrays = {
        "xT": flat.T, "x": flat,
        "wqkv": a["L0_attn_W_qkv"], "abqkv": np.concatenate([a["L0_attn_A_qkv"].T, a["L0_attn_B_qkv"]], 1),
        "wproj": a["L0_attn_W_proj"], "abproj": np.concatenate([a["L0_attn_A_proj"].T, a["L0_attn_B_proj"]], 1),
        "rows": np.concatenate([bq[2 * C:], a["L0_attn_b_proj"], a["L0_ffn_bias"], a["L1_attn_w_dt"]]),
        "cols": np.concatenate([bq[0:C, None], bq[C:2 * C, None], by_block(a["L1_attn_conv_w"]),
                                by_block(a["L1_attn_conv_b"]), by_block(a["L1_attn_D_param"]),
                                by_block(a["L1_attn_b_dt"]), by_block(a["L1_attn_A_log"])], 1),
        "wfp8T": a["L0_ffn_weight_fp8"].T,
        "scales": np.concatenate([a["L0_ffn_input_scale"], a["L0_ffn_weight_scale"]]),
        "win": a["L1_attn_W_in"], "wx": a["L1_attn_W_xproj"], "wout": a["L1_attn_W_out"],
        "rwT": a["L1_ffn_router_w"].T, "w1": a["L1_ffn_w1"],
        "b1c": a["L1_ffn_b1"].reshape(EXPERTS, FB, P).transpose(2, 0, 1),
        "w2": a["L1_ffn_w2"], "b2": a["L1_ffn_b2"],
    }
    arrays = {"in_" + k: np.ascontiguousarray(v) for k, v in arrays.items()}
    nc = bacc.Bacc("TRN2", target_bir_lowering=False, num_devices=1)
    args = [nc.dram_tensor(k, v.shape, F32, kind="ExternalInput").ap() for k, v in arrays.items()]
    N = B * S
    slots = EXPERTS * -(-3 * N // (2 * EXPERTS))
    buf = nc.dram_tensor("slots_in", (slots + N, C), F32, kind="Internal").ap()
    eo = nc.dram_tensor("slots_out", (slots, C), F32, kind="Internal").ap()
    parts = [nc.dram_tensor(f"parts{n}", (HEADS, len(QPARTS), HD, T), BF16, kind="Internal").ap() for n in range(2)]
    out = nc.dram_tensor("out_0", (N, C), F32, kind="ExternalOutput").ap()
    layers(nc, *args, buf, eo, parts, out)
    r = run(nc, [arrays], core_ids=[0])
    return r.results[0]["out_0"].reshape(B, S, C)
```

```python
from contextlib import ExitStack

import concourse.bass as bass
from concourse import mybir

F32 = mybir.dt.float32
BF16 = mybir.dt.bfloat16
I32 = mybir.dt.int32
U32 = mybir.dt.uint32
ALU = mybir.AluOpType
ACT = mybir.ActivationFunctionType
AX = mybir.AxisListType.X

P = 128
EPS = 1e-5
HEADS, HD = 16, 8
PAIRS = HEADS // 2
T = 512
TT = T // P
SEQ = 256
NB = T // SEQ
FP8_MAX = 448.0
STATES = 16
TAPS = 4
DB = 2
NC = 4
CHUNKS = STATES // NC
STEPS = CHUNKS * DB
EXPERTS = 8
FF = 512
FB = FF // P
QPARTS = (0, 1, 2, 0, 1, 0)
KPARTS = (0, 0, 0, 1, 1, 2)
VW = 32
JOBS = HEADS * 2
LAG = 6
LAG_V = LAG + 2
SLOTS_A = 10
SLOTS_F = 10
SPLIT = JOBS - 4
SLOTS_S = 9
STEPS_B = 12
CONSTS = 8
CFRONT, CSPLIT, CCOMMIT, CBACK = 19, 17, 1, 20
STACK = len(QPARTS) * HD


class Chain:

    def __init__(self, eng, sem, stage, per):
        self.eng, self.sem, self.base, self.per, self.n = eng, sem, stage * per, per, 0

    def link(self, ins):
        self.n += 1
        ins.then_inc(self.sem, 1)
        self.eng.wait_ge(self.sem, self.base + self.n)

    def done(self):
        assert self.n == self.per, (self.n, self.per)


def layers(nc, xT_in_d, x_in_d, wqkv_in, aqkvT_in, wproj_in, aprojT_in, rows_in, cols_in, wfp8T_in, scales_in,
           win_in, wx_in, wout_in, rwT_in, w1_in, b1c_in, w2_in, b2_in, buf, eo, parts, bcd, out):
    N = x_in_d.shape[0]
    GROUPS = N // T
    TILES = N // P
    CAP = -(-3 * N // (2 * EXPERTS))
    SLOTS = EXPERTS * CAP
    ST = CAP // P
    assert CAP % P == 0

    with ExitStack() as ctx:
        def sb(name, shape, dt=F32):
            return ctx.enter_context(nc.sbuf_tensor(name, shape, dt))

        def psum(name, shape=(P, 512), dt=F32):
            return ctx.enter_context(nc.psum_tensor(name, list(shape), dt))

        def sem(name):
            return ctx.enter_context(nc.semaphore(name))

        ident = sb("ident", [P, P])
        tri = sb("tri", [P, P], BF16)
        ones = sb("ones", [P, P], BF16)
        wqkv = sb("wqkv", [P, 384])
        wproj = sb("wproj", [P, P])
        aq = sb("aq", [8, P])
        bq = sb("bq", [8, 384])
        ap_ = sb("ap_", [8, P])
        bp = sb("bp", [8, P])
        rows = sb("rows", [P, 3 * P + 2 * P])
        cols = sb("cols", [P, 2 + DB * (TAPS + 3 + STATES)])
        wf = sb("wf", [P, P])
        scales = sb("scales", [P, 2])
        rscale = sb("rscale", [P, 1])
        win = sb("win", [P, 4 * P])
        wx = sb("wx", [P, DB, 33])
        wd = sb("wd", [P, DB, DB * P])
        wout = sb("wout", [P, DB, P])
        rwT = sb("rwT", [P, EXPERTS])
        bqs = sb("bqs", [P, 1])
        aneg = sb("aneg", [P, DB, STATES])
        key8 = sb("key8", [P, TT, EXPERTS])
        key8i = sb("key8i", [P, TT, EXPERTS], I32)
        dump = sb("dump", [P, TT])
        dumpi = sb("dumpi", [P, TT], I32)
        mhalf = sb("mhalf", [P, TT])
        carry = sb("carry", [P, EXPERTS])
        zeros = sb("zeros", [P, P])

        NCOL = 0

        def col(n):
            nonlocal NCOL
            a = cols[:, NCOL:NCOL + n]
            NCOL += n
            return a

        bqc, bkc = col(1), col(1)
        convw = col(DB * TAPS)
        convb, dpar, bdt = col(DB), col(DB), col(DB)
        alog = col(DB * STATES)
        bv_row = rows[:, 0:P]
        bproj_row = rows[:, P:2 * P]
        bff_row = rows[:, 2 * P:3 * P]
        wdt_row = rows[:, 3 * P:5 * P]

        xT = sb("xT", [P, T])
        qparts = sb("qparts", [P, 2, 3, T], BF16)
        qs = sb("qs", [P, NB, PAIRS, SEQ], BF16)
        ks = sb("ks", [P, PAIRS, T], BF16)
        vaug = sb("vaug", [P, TT, HEADS, VW])
        mx = [sb(f"mx{n}", [P, 32], BF16) for n in range(2)]
        mrow = [sb(f"mrow{n}", [32, P], BF16) for n in range(2)]
        probs = sb("probs", [P, 4, 2, SEQ])
        qf = sb("qf", [P, 2, T])
        oq = sb("oq", [P, 4, T])
        xtok = sb("xtok", [P, TT, P])
        rden = sb("rden", [P, TT, HEADS])
        otok = sb("otok", [P, TT, P])
        oT = sb("oT", [P, T])
        x1 = sb("x1", [P, TT, P])
        x2n = sb("x2n", [P, TT, P])
        res = sb("res", [P, TT, P])
        st6 = sb("st6", [P, TT, 6])
        mv = sb("mv", [P, TT, 2])
        vpe = sb("vpe", [P, TT])
        rstd = sb("rstd", [P, TT])
        pre = sb("pre", [P, DB, T])
        qc, qm = pre[:, 0, :], pre[:, 1, :]
        x2T = sb("x2T", [P, T])
        xq = x2T[:]
        xpad = sb("xpad", [P, DB, NB, SEQ + TAPS - 1])
        cacc = sb("cacc", [P, DB, T])
        xn = sb("xn", [P, DB, T])
        szn = sb("szn", [P, DB, T])
        bcf = sb("bcf", [2 * STATES, T])
        x2 = sb("x2", [P, TT, P])
        xc = sb("xc", [P, DB, T])
        sz = sb("sz", [P, DB, T])
        dlt = sb("dlt", [P, DB, T])
        dx = sb("dx", [P, DB, T])
        brep = [sb(f"brep{n}", [P, NC, T]) for n in range(2)]
        crep = [sb(f"crep{n}", [P, NC, T]) for n in range(2)]
        da = [sb(f"da{n}", [P, NC, T]) for n in range(2)]
        u = [sb(f"u{n}", [P, NC, T]) for n in range(3)]
        yg = u[2][:, 0:DB, :]
        x3 = sb("x3", [P, TT, P])
        x3T = x2T
        x3all = sb("x3all", [P, TILES, P])
        lg = sb("lg", [P, TT, EXPERTS])
        lge = sb("lge", [P, TT, EXPERTS])
        oh = sb("oh", [P, TT, EXPERTS], BF16)
        r4 = sb("r4", [P, 8, TT])
        sidx = sb("sidx", [P, TT], U32)
        gidx = sb("gidx", [P, TILES], U32)
        gate = sb("gate", [P, TILES])

        w1s = [da[0][:, n, :] for n in range(2)]
        w2s = [da[0][:, 2 + n, :].rearrange("p (f d) -> p f d", d=P) for n in range(2)]
        b2s = [da[1][:, 0, n * P:(n + 1) * P] for n in range(2)]
        xe = [da[1][:, 1 + n, 0:CAP].rearrange("p (t c) -> p t c", c=P) for n in range(2)]
        xeT = [da[1][:, 3, 0:CAP], u[0][:, 0, 0:CAP]]
        hT = [u[0][:, 1, 0:CAP], u[0][:, 2, 0:CAP], u[0][:, 3, 0:CAP], u[1][:, 0, 0:CAP]]
        ye = [u[1][:, 1 + n, 0:CAP].rearrange("p (t c) -> p t c", c=P) for n in range(2)]
        b1c = sb("b1c", [P, EXPERTS, FB])
        yall = brep[0][:].rearrange("p n t -> p (n t)").rearrange("p (t c) -> p t c", c=P)

        E = [psum("E0"), psum("E1")]
        M = [psum("M0"), psum("M1")]
        V = psum("V")
        GF = psum("GF")
        Y = [psum("Y0"), psum("Y1")]

        wa_in = sem("wa_in")
        w_in = sem("w_in")
        zeroed = sem("zeroed")
        consts = sem("consts")
        prep_pe, prep_act, prep_dve = sem("prep_pe"), sem("prep_act"), sem("prep_dve")
        xT_in, x_in = sem("xT_in"), sem("x_in")
        qkv_mm = sem("qkv_mm")
        parts_ready = sem("parts_ready")
        vaug_ready = sem("vaug_ready")
        q_read, q_split = sem("q_read"), sem("q_split")
        parts_out = sem("parts_out")
        stack_in = [sem("stack_in0"), sem("stack_in1")]
        max_mm, max_read = sem("max_mm"), sem("max_read")
        mrow_ready = sem("mrow_ready")
        mrow_in = [sem("mrow_in0"), sem("mrow_in1")]
        qk_mm, exp_done, pv_mm = sem("qk_mm"), sem("exp_done"), sem("pv_mm")
        ov_read = sem("ov_read")
        f_pe, f_act, f_dve, f_pool = sem("f_pe"), sem("f_act"), sem("f_dve"), sem("f_pool")
        FPE, FACT, FDVE, FPOOL = 16, 12, 9, 2
        varf_ready, rstdf_ready = sem("varf_ready"), sem("rstdf_ready")
        varb_ready, rstdb_ready = sem("varb_ready"), sem("rstdb_ready")
        committed = sem("committed")
        bc_out = sem("bc_out")
        b_in = [sem("b_in0"), sem("b_in1")]
        c_in = [sem("c_in0"), sem("c_in1")]
        da_ready = sem("da_ready")
        u_ready = sem("u_ready")
        a_ready = sem("a_ready")
        h_ready = sem("h_ready")
        scanned = sem("scanned")
        y_mm = sem("y_mm")
        y_in = sem("y_in")
        b_pe, b_act, b_dve = sem("b_pe"), sem("b_act"), sem("b_dve")
        BPE, BACT, BDVE = 4, 3, 5
        scattered = sem("scattered")
        c_att, c_front, c_back = sem("c_att"), sem("c_front"), sem("c_back")
        c_commit = sem("c_commit")
        b1_in = sem("b1_in")
        passed = sem("passed")
        we_in = [sem("we_in0"), sem("we_in1")]
        tok_in = [sem("tok_in0"), sem("tok_in1")]
        eo_out = [sem("eo_out0"), sem("eo_out1")]
        e_pe, e_act, e_dve = sem("e_pe"), sem("e_act"), sem("e_dve")
        EPE, EACT = 2 + FB, 1 + FB
        gathered = [sem(f"gathered{g}") for g in range(GROUPS)]
        z_dve = sem("z_dve")
        out_done = sem("out_done")

        block = ctx.enter_context(nc.Block())
        LOADS_A, LOADS = 5, 9
        PREP_DVE = 17

        def wait(eng, signal, count):
            if not isinstance(count, int) or count > 0:
                eng.wait_ge(signal, count)

        def wait_apart(eng, signal, count):
            wait(eng, signal, count)
            eng.sem_inc(passed, 1)

        def is_first(g):
            return isinstance(g, int) and g == 0

        def stages(eng, phase, between):
            between(0, None, None)
            phase(0, 0, None, None)
            phase(1, 0, None, None, 1)
            between(1, None, None)
            phase(0, 1, 0, None)
            phase(1, 1, 0, None, 2)
            between(2, None, 0)
            phase(0, 2, 1, 0)
            with eng.Fori(1, GROUPS - 2) as g:
                phase(1, g + 1, g, g - 1, g + 2)
                between(g + 2, g - 1, g)
                phase(0, g + 2, g + 1, g)
            phase(1, GROUPS - 1, GROUPS - 2, GROUPS - 3)
            between(None, GROUPS - 3, GROUPS - 2)
            phase(0, None, GROUPS - 1, GROUPS - 2)
            phase(1, None, GROUPS - 1, GROUPS - 2)
            between(None, GROUPS - 2, GROUPS - 1)
            phase(0, None, None, GROUPS - 1)
            phase(1, None, None, GROUPS - 1)
            between(None, GROUPS - 1, None)

        def back_of(s_):
            return None if s_ is None or is_first(s_) else s_ - 1

        def subslots(part, a, f, s_):
            n = max(SLOTS_A if a is not None else 0, SLOTS_F if f is not None else 0, SLOTS_S if s_ is not None else 0)
            return [(t, t // 4, t % 4) for t in (range(SPLIT) if part == 0 else range(SPLIT, 4 * n))]

        def up_count(e, f):
            return 1 + EPE * e + f + 1

        def turn_count(e):
            return 1 if e == 0 else 1 + EPE * (e - 1) + FB + 1

        def down_count(e):
            return 1 + EPE * e + FB + (2 if e + 1 < EXPERTS else 1)

        @block.sync
        def _(sp):
            def load(signal, *pairs):
                for dst, src in pairs:
                    sp.dma_start(dst, src).then_inc(signal, 16)

            load(wa_in, (wqkv[:], wqkv_in), (aq[:], aqkvT_in[:, 0:P]), (bq[:], aqkvT_in[:, P:]), (cols[:], cols_in),
                 (rows[:], rows_in.partition_broadcast(P)))

            def load_rest():
                load(w_in, (wproj[:], wproj_in), (ap_[:], aprojT_in[:, 0:P]), (bp[:], aprojT_in[:, P:]),
                     (wf[:], wfp8T_in), (scales[:], scales_in.partition_broadcast(P)), (win[:], win_in),
                     (wx[:], wx_in.rearrange("(b p) n -> p b n", p=P)),
                     (wout[:], wout_in.rearrange("(b p) n -> p b n", p=P)), (rwT[:], rwT_in))
                sp.wait_ge(consts, CONSTS)
                for r in range(SLOTS // P):
                    sp.dma_start(buf[r * P:(r + 1) * P, :], zeros[:]).then_inc(zeroed, 16)

            def load_states(s_, c, which):
                dst, signal = (brep, crep)[which][c % 2], (b_in, c_in)[which][c % 2]
                row = which * STATES + NC * c
                if c >= 2 and which == 0:
                    wait_apart(sp, u_ready, 3 * (8 * s_ + 2 * (c - 1)))
                if c >= 2 and which == 1:
                    wait_apart(sp, h_ready, 2 * (8 * s_ + 2 * (c - 1)))
                sp.dma_start(dst[:], bcd[bass.ds(s_, 1), row:row + NC, :].rearrange("o n t -> o (n t)")
                                 .to_broadcast([P, NC * T]).rearrange("p (n t) -> p n t", n=NC)).then_inc(signal, 16)

            def load_x(a):
                wait_apart(sp, qkv_mm, 3 * a)
                sp.dma_start(xT[:], xT_in_d[:, bass.ds(a * T, T)]).then_inc(xT_in, 16)

            def store_part(a, r):
                if r < 2:
                    sp.wait_ge(q_read, 4 * a + 3 + r)
                else:
                    sp.wait_ge(parts_ready, a + 1)
                for n, order in enumerate((QPARTS, KPARTS)):
                    for m, part in enumerate(order):
                        if part == r:
                            sp.dma_start(parts[n][:, m], qparts[:, n, r, :]).then_inc(parts_out, 16)

            def load_stacks(a):
                wait_apart(sp, parts_out, 16 * 2 * len(QPARTS) * (a + 1))
                wait_apart(sp, qk_mm, 32 * a)
                if is_first(a):
                    sp.wait_ge(prep_dve, 5)
                for i in range(2):
                    q_rows, k_rows = (parts[n].rearrange("(j i) n d t -> i (n d) j t", i=2)[i] for n in range(2))
                    for b in range(NB):
                        sp.dma_start(qs[64 * i:64 * i + STACK, b], q_rows[:, :, b * SEQ:(b + 1) * SEQ]
                                     ).then_inc(stack_in[i], 16)
                    sp.dma_start(ks[64 * i:64 * i + STACK], k_rows).then_inc(stack_in[i], 16)

            def between(a, g, f):
                if is_first(a):
                    load_x(a)
                    load_rest()
                    for r in range(3):
                        store_part(a, r)
                if f is not None:
                    wait_apart(sp, bc_out, 16 * (f + 1))
                    wait_apart(sp, h_ready, 2 * 8 * f)
                    load_states(f, 0, 0)
                if a is not None:
                    load_stacks(a)
                if f is not None:
                    load_states(f, 0, 1)
                    load_states(f, 1, 0)
                    load_states(f, 1, 1)

            def phase(part, a, f, s_, nxt=None):
                if f is not None and part == 0:
                    wait_apart(sp, committed, f)
                    sp.dma_start(xtok[:], x_in_d[bass.ds(f * T, T), :].rearrange("(t p) c -> p t c", p=P)
                                 ).then_inc(x_in, 16)
                if nxt is not None:
                    load_x(nxt)
                for t, k, n in subslots(part, a, f, s_):
                    if n == 3 and a is not None and k < 8:
                        q = k
                        b, j = q // 4, 2 * (q % 4)
                        sp.wait_ge(mrow_ready, 8 * a + q + 1)
                        for i in range(2):
                            dst = qs[64 * i + STACK:64 * i + STACK + 1, b, j:j + 2, :]
                            sp.dma_start(dst.rearrange("o j (a t) -> o (j a) t", a=2),
                                         mrow[q % 2][4 * i:4 * i + 4, :]).then_inc(mrow_in[q % 2], 16)
                    if n == 3 and s_ is not None and k in (1, 3):
                        load_states(s_, (k + 3) // 2, 0)
                        load_states(s_, (k + 3) // 2, 1)
                if nxt is not None:
                    store_part(nxt, 0)
                    store_part(nxt, 1)
                if f is not None and part == 1:
                    sp.wait_ge(f_act, FACT * f + 8)
                    sp.dma_start(bcd[bass.ds(f, 1), :, :].rearrange("o n t -> (o n) t"), bcf[:]).then_inc(bc_out, 16)
                if nxt is not None:
                    store_part(nxt, 2)

            stages(sp, phase, between)

            sp.wait_ge(y_mm, 8 * GROUPS)
            for e in range(EXPERTS):
                w = e % 2

                if e >= 2:
                    sp.wait_ge(e_pe, turn_count(e - 2))
                    sp.dma_start(xe[w], buf[e * CAP:(e + 1) * CAP, :].rearrange("(t p) c -> p t c", p=P)
                                 ).then_inc(tok_in[w], 16)
                    sp.wait_ge(e_pe, down_count(e - 2))
                    sp.wait_ge(e_dve, e - 1)
                sp.dma_start(w1s[w], w1_in[e]).then_inc(we_in[w], 16)
                sp.dma_start(w2s[w], w2_in[e].rearrange("(f p) d -> p f d", p=P)).then_inc(we_in[w], 16)
                sp.dma_start(b2s[w], b2_in[e].partition_broadcast(P)).then_inc(we_in[w], 16)
                if e == 1:
                    sp.wait_ge(scattered, 16 * TILES)
                    for w in range(2):
                        sp.dma_start(xe[w], buf[w * CAP:(w + 1) * CAP, :].rearrange("(t p) c -> p t c", p=P)
                                     ).then_inc(tok_in[w], 16)
            for g in range(GROUPS):
                sp.wait_ge(z_dve, g + 1)
                sp.dma_start(out[g * T:(g + 1) * T, :].rearrange("(t p) c -> p t c", p=P),
                             x3all[:, g * TT:(g + 1) * TT, :]).then_inc(out_done, 16)
            sp.wait_ge(out_done, 16 * GROUPS)

        @block.tensor
        def _(pe):
            pe.wait_ge(wa_in, 16 * LOADS_A)
            pe.matmul(E[0][:, 0:384], aq[:], bq[:], start=True, stop=True).then_inc(prep_pe, 1)
            pe.wait_ge(prep_dve, 2)

            def turn(dst, src, n=TT):
                for t in range(n):
                    last = pe.transpose(dst[:, t * P:(t + 1) * P], src[:, t, :], ident[:])
                return last

            def attend_qk(a):
                pe.wait_ge(xT_in, 16 * (a + 1))
                wait(pe, max_read, 32 * a - 1)
                pe.matmul(M[0][:], wqkv[:, 0:P], xT[:], start=True, stop=True).then_inc(qkv_mm, 1)
                wait(pe, max_read, 32 * a)
                pe.matmul(M[1][:], wqkv[:, P:2 * P], xT[:], start=True, stop=True).then_inc(qkv_mm, 1)

            def attend_v(a):
                wait(pe, ov_read, 8 * a)
                for t in range(TT):
                    last = pe.matmul(V[:, t * P:(t + 1) * P], xT[:, t * P:(t + 1) * P], wqkv[:, 2 * P:],
                                     start=True, stop=True)
                last.then_inc(qkv_mm, 1)

            def max_head(a, q, n):
                b, j, i = q // 4, 2 * (q % 4) + n // 2, n % 2
                if q == 0 and n == 0:
                    wait(pe, q_read, 4 * a + 2)
                if q == 0 and n < 2:
                    pe.wait_ge(stack_in[n], 16 * 3 * (a + 1))
                wait(pe, max_read, 32 * a + 4 * q + n - 1)
                at = slice(64 * i, 64 * i + STACK)
                for t in range(2):
                    last = pe.matmul(M[n % 2][:, t * SEQ:(t + 1) * SEQ],
                                     qs[at, b, j, t * P:(t + 1) * P],
                                     ks[at, j, b * SEQ:(b + 1) * SEQ], start=True, stop=True)
                last.then_inc(max_mm, 1)

            def score_head(a, q, n):
                b, j, i = q // 4, 2 * (q % 4) + n // 2, n % 2
                h = 32 * a + 4 * q + n
                if n == 0:
                    pe.wait_ge(mrow_in[q % 2], 32 * (4 * a + q // 2 + 1))
                wait(pe, exp_done, h - 1)
                at = slice(64 * i, 64 * i + STACK + 1)
                for t in range(2):
                    last = pe.matmul(E[n % 2][:, t * SEQ:(t + 1) * SEQ],
                                     ks[at, j, b * SEQ + t * P:b * SEQ + (t + 1) * P],
                                     qs[at, b, j, :], start=True, stop=True)
                last.then_inc(qk_mm, 1)

            def value_head(a, q, n):
                b, h = q // 4, 4 * (q % 4) + n
                pe.wait_ge(exp_done, 32 * a + 4 * q + n + 1)
                if n == 0:
                    if q == 0:
                        pe.wait_ge(vaug_ready, a + 1)
                    wait(pe, ov_read, 8 * a + q)
                for kt in range(2):
                    last = pe.matmul(V[VW * n:VW * (n + 1), 0:SEQ], vaug[:, 2 * b + kt, h, :], probs[:, n, kt, :],
                                     start=(kt == 0), stop=(kt == 1))
                last.then_inc(pv_mm, 1)

            def states_sum(g, st, n, count):
                c, db = st // DB, st % DB
                if count == NC and n % 2 == 0:
                    pe.wait_ge(h_ready, 2 * (8 * g + st) + n // 2 + 1)
                if count < NC and n == 0:
                    pe.wait_ge(a_ready, 8 * g + st + 1)
                    if st == 1:
                        wait(pe, b_dve, BDVE * (g - 1) + 5)
                last = pe.matmul(Y[db][:], ident[:], u[st % 3][:, n, :], start=(c == 0 and n == 0),
                                 stop=(c == CHUNKS - 1 and n == count - 1), skip_group_check=True)
                if n == count - 1:
                    last.then_inc(y_mm, 1)

            def front(g, t):
                F, A, D = FPE * g, FACT * g, FDVE * g
                if t in (0, 1, 2, 3):
                    tt = t
                    if t == 0:
                        wait(pe, ov_read, 8 * (g + 1))
                        wait(pe, f_act, A)
                    else:
                        pe.wait_ge(f_dve, D + tt)
                    turn(GF, oq[:, :, tt * P:(tt + 1) * P]).then_inc(f_pe, 1)
                if t == 4:
                    pe.wait_ge(f_dve, D + 4)
                    turn(GF, otok).then_inc(f_pe, 1)
                if t == 6:
                    pe.wait_ge(f_act, A + 1)
                    for m in range(TT):
                        last = pe.matmul(GF[:, m * P:(m + 1) * P], oT[:, m * P:(m + 1) * P], wproj[:],
                                         start=True, stop=True)
                    last.then_inc(f_pe, 1)
                if t == 12:
                    pe.wait_ge(f_dve, D + 5)
                    turn(GF, x1).then_inc(f_pe, 1)
                if t == 16:
                    pe.wait_ge(f_dve, D + 6)
                    for m in range(TT):
                        last = pe.matmul(GF[:, m * P:(m + 1) * P], xq[:, m * P:(m + 1) * P], wf[:],
                                         start=True, stop=True)
                    last.then_inc(f_pe, 1)
                if t == 22:
                    pe.wait_ge(f_dve, D + 7)
                    turn(GF, x2n).then_inc(f_pe, 1)
                if t in (24, 26, 28, 30):
                    n = (t - 24) // 2
                    pe.wait_ge(f_act, A + 2 + n)
                    pe.matmul(GF[:], win[:, n * P:(n + 1) * P], x2T[:], start=True, stop=True
                              ).then_inc(f_pe, 1)
                if t == 33:
                    pe.wait_ge(f_act, A + 7)
                    for eb in range(DB):
                        last = pe.matmul(GF[0:32, :], wx[:, eb, 1:33], xn[:, eb, :], start=(eb == 0), stop=(eb == 1))
                    last.then_inc(f_pe, 1)
                if t in (35, 37):
                    db = (t - 35) // 2
                    pe.wait_ge(f_act, A + 8 + db)
                    for eb in range(DB):
                        last = pe.matmul(GF[:], wd[:, eb, db * P:(db + 1) * P], xn[:, eb, :],
                                         start=(eb == 0), stop=(eb == 1))
                    last.then_inc(f_pe, 1)

            def back(g, t, W):
                if t == 0:
                    pe.wait_ge(b_dve, BDVE * g + 1)
                    for m in range(TT):
                        for db in range(DB):
                            last = pe.matmul(W[:, m * P:(m + 1) * P], yg[:, db, m * P:(m + 1) * P], wout[:, db, :],
                                             start=(db == 0), stop=(db == 1))
                    last.then_inc(b_pe, 1)
                if t == 4:
                    pe.wait_ge(b_dve, BDVE * g + 2)
                    turn(W, x3).then_inc(b_pe, 1)
                if t == 5:
                    pe.wait_ge(b_act, BACT * g + 1)
                    for m in range(TT):
                        last = pe.matmul(W[:, m * 8:(m + 1) * 8], x3T[:, m * P:(m + 1) * P], rwT[:],
                                         start=True, stop=True)
                    last.then_inc(b_pe, 1)
                if t == 8:
                    pe.wait_ge(b_dve, BDVE * g + 4)
                    counts = W[:, 0:TT * EXPERTS].rearrange("p (t e) -> p t e", t=TT)
                    pe.matmul(counts, tri[:], oh[:], start=True, stop=False, skip_group_check=True)
                    for v in range(TT - 1):
                        pe.matmul(counts[:, v + 1:], ones[:], oh[:, v:v + 1, :].to_broadcast([P, TT - 1 - v, EXPERTS]),
                                  start=False, stop=(v == TT - 2), skip_group_check=True)
                    for m in range(TT):
                        last = pe.matmul(W[:, 32:40], ones[:], oh[:, m, :], start=(m == 0), stop=(m == TT - 1))
                    last.then_inc(b_pe, 1)

            def phase(part, a, f, s_, nxt=None):
                for t, k, n in subslots(part, a, f, s_):
                    if a is not None:
                        if t < JOBS:
                            max_head(a, t // 4, t % 4)
                        if 0 <= t - LAG < JOBS:
                            score_head(a, (t - LAG) // 4, (t - LAG) % 4)
                        if 0 <= t - LAG_V < JOBS:
                            value_head(a, (t - LAG_V) // 4, (t - LAG_V) % 4)
                    if s_ is not None:
                        if a is None and 2 <= t < 34:
                            states_sum(s_, (t - 2) // 4, (t - 2) % 4, NC)
                        if a is not None and 1 <= k <= 8 and n >= 2:
                            states_sum(s_, k - 1, n - 2, 2)
                    if f is not None:
                        front(f, t)
                    if back_of(s_) is not None:
                        back(back_of(s_), t, Y[1] if a is not None else M[1])
                    if nxt is not None and t == JOBS:
                        attend_qk(nxt)

            def between(a, g, f):
                if is_first(a):
                    attend_qk(a)
                if a is not None:
                    attend_v(a)
                if is_first(a):
                    pe.wait_ge(w_in, 16 * LOADS)
                    pe.matmul(GF[:, 0:P], ap_[:], bp[:], start=True, stop=True).then_inc(prep_pe, 1)
                    pe.wait_ge(consts, CONSTS)
                    pe.wait_ge(prep_dve, PREP_DVE)
                if g is not None and f is None:
                    for t in range(STEPS_B):
                        back(g, t, M[1])

            stages(pe, phase, between)

            def e_turn(e):
                pe.wait_ge(tok_in[e % 2], 16 * (e // 2 + 1))
                if e >= 2:
                    pe.wait_ge(e_act, EACT * (e - 2) + 1)
                turn((GF, M[1])[e % 2], xe[e % 2], ST).then_inc(e_pe, 1)

            pe.wait_ge(b_dve, BDVE * GROUPS)
            e_turn(0)
            for e in range(EXPERTS):
                w = e % 2
                pe.wait_ge(we_in[w], 48 * (e // 2 + 1))
                pe.wait_ge(e_act, EACT * e + 1)
                for f, bank in enumerate((E[0], E[1], M[0], V)):
                    if e >= 1:
                        pe.wait_ge(e_act, EACT * (e - 1) + 2 + f)
                    pe.matmul(bank[:, 0:CAP], w1s[w][:, f * P:(f + 1) * P], xeT[w], start=True, stop=True
                              ).then_inc(e_pe, 1)
                if e + 1 < EXPERTS:
                    e_turn(e + 1)
                pe.wait_ge(e_act, EACT * e + 1 + FB)
                if e >= 2:
                    pe.wait_ge(e_dve, e - 1)
                for t in range(ST):
                    for f in range(FB):
                        last = pe.matmul(Y[w][:, t * P:(t + 1) * P], hT[f][:, t * P:(t + 1) * P], w2s[w][:, f, :],
                                         start=(f == 0), stop=(f == FB - 1))
                last.then_inc(e_pe, 1)

        @block.scalar
        def _(act):
            act.dma_start(b1c[:], b1c_in).then_inc(b1_in, 16)
            act.wait_ge(wa_in, 16 * LOADS_A)
            act.activation(aneg[:].rearrange("p b n -> p (b n)"), alog, ACT.Exp).then_inc(prep_act, 1)

            def attend_pre(a, step):
                if step == 0:
                    wait(act, parts_ready, a)
                    act.wait_ge(qkv_mm, 3 * a + 1)
                    act.activation(qf[:, 0, :], M[0][:], ACT.Identity, bias=bqs[:, 0:1], scale=HD ** -0.5
                                   ).then_inc(q_read, 1)
                    act.wait_ge(qkv_mm, 3 * a + 2)
                    act.activation(qf[:, 1, :], M[1][:], ACT.Identity, bias=bkc).then_inc(q_read, 1)
                if step == 1:
                    wait(act, parts_out, 16 * 2 * len(QPARTS) * a)
                    act.wait_ge(q_read, 4 * a + 2)
                    act.copy(qparts[:, :, 0, :], qf[:]).then_inc(q_read, 1)
                if step == 2:
                    act.wait_ge(q_split, a + 1)
                    act.copy(qparts[:, :, 1, :], qf[:]).then_inc(q_read, 1)

            def exp_head(a, q, n):
                h = 32 * a + 4 * q + n
                act.wait_ge(qk_mm, h + 1)
                wait(act, pv_mm, h - 3)
                act.activation(probs[:, n].rearrange("p k t -> p (k t)"), E[n % 2][:], ACT.Exp).then_inc(exp_done, 1)

            def read_values(a, q):
                act.wait_ge(pv_mm, 32 * a + 4 * q + 4)
                if q == 0:
                    wait(act, f_pe, FPE * (a - 1) + 4)
                b = q // 4
                act.copy(oq[:, q % 4, b * SEQ:(b + 1) * SEQ], V[:, 0:SEQ]).then_inc(ov_read, 1)

            def decay(g, st, n):
                c, db = st // DB, st % DB
                if st == 0 and n == 0:
                    act.wait_ge(committed, g + 1)
                if st >= 2 and n == 0:
                    act.wait_ge(scanned, 2 * (8 * g + st - 1))
                last = act.activation(da[st % 2][:, n, :], dlt[:, db, :], ACT.Exp,
                                      scale=aneg[:, db, NC * c + n:NC * c + n + 1])
                if n == NC - 1:
                    last.then_inc(da_ready, 1)

            def front(g, t):
                F = FPE * g
                if t == 5:
                    act.wait_ge(f_pe, F + 5)
                    act.copy(oT[:], GF[:]).then_inc(f_act, 1)
                if t == 23:
                    act.wait_ge(f_pe, F + 9)
                    act.copy(x2T[:], GF[:]).then_inc(f_act, 1)
                if t in (25, 27):
                    db = (t - 25) // 2
                    act.wait_ge(f_pe, F + 10 + db)
                    act.copy(xpad[:, db, :, TAPS - 1:], GF[:].rearrange("p (b t) -> p b t", b=NB)
                             ).then_inc(f_act, 1)
                if t in (29, 31):
                    db = (t - 29) // 2
                    act.wait_ge(f_pe, F + 12 + db)
                    act.copy(szn[:, db, :], GF[:]).then_inc(f_act, 1)
                if t == 32:
                    act.wait_ge(f_act, FACT * g + 6)
                    act.activation(szn[:], szn[:], ACT.Silu)
                    act.wait_ge(f_dve, FDVE * g + 8)
                    act.activation(xn[:], cacc[:], ACT.Silu).then_inc(f_act, 1)
                if t == 34:
                    act.wait_ge(f_pe, F + 14)
                    act.copy(bcf[:], GF[0:32, :]).then_inc(f_act, 1)
                if t in (36, 38):
                    db = (t - 36) // 2
                    act.wait_ge(f_pe, F + 15 + db)
                    act.activation(pre[:, db, :], GF[:], ACT.Identity, bias=bdt[:, db:db + 1]).then_inc(f_act, 1)
                if t == 39:
                    act.wait_ge(f_dve, FDVE * g + 9)
                    act.activation(cacc[:], cacc[:], ACT.Exp).then_inc(f_act, 1)
                    act.wait_ge(f_act, FACT * g + 11)
                    act.activation(cacc[:], cacc[:], ACT.Ln, bias=1.0).then_inc(f_act, 1)

            def back(g, t, W):
                if t == 4:
                    act.wait_ge(b_pe, BPE * g + 2)
                    act.copy(x3T[:], W[:]).then_inc(b_act, 1)
                if t == 6:
                    act.wait_ge(b_dve, BDVE * g + 3)
                    act.activation(lge[:], lg[:], ACT.Exp).then_inc(b_act, 1)
                    act.copy(x3all[:, bass.ds(g * TT, TT), :], x3[:]).then_inc(b_act, 1)

            def phase(part, a, f, s_, nxt=None):
                for t, k, n in subslots(part, a, f, s_):
                    if a is not None:
                        v = t - LAG_V - 4
                        if v >= 0 and v % 4 == 0:
                            read_values(a, v // 4)
                        if 0 <= t - LAG < JOBS:
                            exp_head(a, (t - LAG) // 4, (t - LAG) % 4)
                        if t == LAG_V + JOBS - 1:
                            read_values(a, JOBS // 4 - 1)
                    if s_ is not None:
                        if k < 7:
                            decay(s_, k + 1, n)
                    if f is not None:
                        front(f, t)
                    if back_of(s_) is not None:
                        back(back_of(s_), t, Y[1] if a is not None else M[1])
                    if nxt is not None and JOBS <= t < JOBS + 3:
                        attend_pre(nxt, t - JOBS)

            def between(a, g, f):
                if is_first(a):
                    for step in range(3):
                        attend_pre(a, step)
                if f is not None:
                    for n in range(NC):
                        decay(f, 0, n)
                if g is not None and f is None:
                    for t in range(STEPS_B):
                        back(g, t, M[1])

            stages(act, phase, between)

            act.wait_ge(b1_in, 16)
            for e in range(EXPERTS):
                act.wait_ge(e_pe, turn_count(e))
                act.copy(xeT[e % 2], (GF, M[1])[e % 2][:, 0:CAP]).then_inc(e_act, 1)
                for f, bank in enumerate((E[0], E[1], M[0], V)):
                    act.wait_ge(e_pe, up_count(e, f))
                    if e >= 1 and f == 0:
                        act.wait_ge(e_pe, down_count(e - 1))
                    act.activation(hT[f], bank[:, 0:CAP], ACT.Gelu, bias=b1c[:, e, f:f + 1]).then_inc(e_act, 1)

        @block.vector
        def _(dve):
            prep = Chain(dve, prep_dve, 0, PREP_DVE)
            dve.wait_ge(wa_in, 16 * LOADS_A)
            prep.link(dve.tensor_scalar(bqs[:], bqc, HD ** -0.5, None, ALU.mult))
            dve.wait_ge(prep_pe, 1)
            prep.link(dve.scalar_tensor_tensor(wqkv[:], E[0][:, 0:384], 2.0, wqkv[:], ALU.mult, ALU.add))
            prep.link(dve.memset(vaug[:], 0.0))
            prep.link(dve.memset(vaug[:, :, :, HD:HD + 1], 1.0))

            def prepare_rest():
                prep.link(dve.memset(ks[:], 1.0))
                for n in range(2):
                    prep.link(dve.memset(mx[n][:], 0.0))
                dve.wait_ge(w_in, 16 * LOADS)
                dve.wait_ge(consts, CONSTS)
                dve.wait_ge(prep_act, 1)
                prep.link(dve.tensor_scalar(aneg[:], aneg[:], -1.0, None, ALU.mult))
                for eb in range(DB):
                    prep.link(dve.tensor_scalar(wd[:, eb, :], wdt_row, wx[:, eb, 0:1], None, ALU.mult))
                prep.link(dve.tensor_scalar(wf[:], wf[:], scales[:, 0:1], scales[:, 1:2], ALU.mult, ALU.mult))
                prep.link(dve.reciprocal(rscale[:], scales[:, 0:1]))
                prep.link(dve.tensor_copy(key8[:], key8i[:]))
                prep.link(dve.tensor_copy(dump[:], dumpi[:]))
                prep.link(dve.memset(carry[:], 0.0))
                prep.link(dve.memset(xpad[:], 0.0))
                dve.wait_ge(prep_pe, 2)
                prep.link(dve.scalar_tensor_tensor(wproj[:], GF[:, 0:P], 2.0, wproj[:], ALU.mult, ALU.add))
                prep.done()

            def norm_stats(ch, ready):
                for t in range(TT):
                    last = dve.bn_stats(st6[:, t, :], res[:, t, :])
                ch.n += 1
                last.then_inc(ch.sem, 1)
                wait_apart(dve, ch.sem, ch.base + ch.n)
                for t in range(TT):
                    last = dve.bn_aggr(mv[:, t, :], st6[:, t, :])
                ch.link(last)
                dve.tensor_scalar(vpe[:], mv[:, :, 1], EPS, None, ALU.add).then_inc(ready, 1)

            def norm_apply(signal, count, dst):
                dve.wait_ge(signal, count)
                for t in range(TT):
                    last = dve.tensor_scalar(dst[:, t, :], res[:, t, :], mv[:, t, 0:1], rstd[:, t:t + 1],
                                             ALU.subtract, ALU.mult)
                return last

            def attend_split(a, step):
                if step == 0:
                    dve.wait_ge(q_read, 4 * a + 3)
                    dve.tensor_tensor(qf[:], qf[:], qparts[:, :, 0, :], ALU.subtract).then_inc(q_split, 1)
                if step == 1:
                    dve.wait_ge(q_read, 4 * a + 4)
                    dve.wait_ge(q_split, a + 1)
                    dve.tensor_tensor(qparts[:, :, 2, :], qf[:], qparts[:, :, 1, :], ALU.subtract
                                      ).then_inc(parts_ready, 1)

            def attend_v(a):
                dve.wait_ge(qkv_mm, 3 * a + 3)
                dve.tensor_tensor(vaug[:, :, :, 0:HD], V[:].rearrange("p (t h d) -> p t h d", t=TT, d=HD),
                                  bv_row.rearrange("p (h d) -> p h d", d=HD).unsqueeze(1)
                                  .to_broadcast([P, TT, HEADS, HD]), ALU.add).then_inc(vaug_ready, 1)

            def head_max(a, q, n):
                dve.wait_ge(max_mm, 32 * a + 4 * q + n + 1)
                c = 4 * (n % 2) + 2 * (n // 2)
                dve.tensor_reduce(mx[q % 2][:, c:c + 2], M[n % 2][:].rearrange("p (t k) -> p t k", t=2), AX, ALU.max,
                                  negate=True).then_inc(max_read, 1)

            def max_rows(a, q):
                dve.wait_ge(max_read, 32 * a + 4 * q + 4)
                wait(dve, mrow_in[q % 2], 32 * (4 * a + q // 2))
                for m in range(P // 32):
                    at = slice(32 * m, 32 * (m + 1))
                    last = dve.transpose(mrow[q % 2][:, at], mx[q % 2][at, :])
                last.then_inc(mrow_ready, 1)

            def scan_half(g, st, half):
                at = slice(2 * half, 2 * half + 2)
                if half == 0:
                    dve.wait_ge(u_ready, 3 * (8 * g + st + 1))
                ub = u[st % 3][:, at, :].rearrange("p n t -> p (n t)")
                dve.tensor_tensor_scan(ub, da[st % 2][:, at, :].rearrange("p n t -> p (n t)"), ub, 0.0,
                                       ALU.mult, ALU.add).then_inc(scanned, 1)

            def gate_half(g, st, half):
                c, at = st // DB, slice(2 * half, 2 * half + 2)
                dve.wait_ge(scanned, 2 * (8 * g + st) + half + 1)
                if half == 0:
                    dve.wait_ge(c_in[c % 2], 16 * (2 * g + c // 2 + 1))
                dve.tensor_tensor(u[st % 3][:, at, :], u[st % 3][:, at, :], crep[c % 2][:, at, :], ALU.mult
                                  ).then_inc(h_ready, 1)

            def front(g, t, ch):
                F, A, D = FPE * g, FACT * g, FDVE * g
                flat = lambda a: a.rearrange("p t c -> p (t c)")
                if t in (0, 1, 2, 3):
                    tt = t
                    dve.wait_ge(f_pe, F + tt + 1)
                    v = GF[:].rearrange("p (h w) -> p h w", w=VW)
                    ch.link(dve.reciprocal(rden[:, tt, :], v[:, :, HD]))
                    dve.tensor_tensor(otok[:, tt, :].rearrange("p (h d) -> p h d", d=HD), v[:, :, 0:HD],
                                      rden[:, tt, :].unsqueeze(2).to_broadcast([P, HEADS, HD]), ALU.mult
                                      ).then_inc(f_dve, 1)
                if t == 7:
                    dve.wait_ge(f_pe, F + 6)
                    dve.wait_ge(f_pool, FPOOL * g + 1)
                    ch.link(dve.tensor_tensor(flat(res[:]), GF[:], flat(xtok[:]), ALU.add))
                    norm_stats(ch, varf_ready)
                if t == 11:
                    norm_apply(rstdf_ready, 2 * g + 1, x1).then_inc(f_dve, 1)
                if t == 13:
                    dve.wait_ge(f_pe, F + 7)
                    ch.link(dve.tensor_scalar(qc, GF[:], rscale[:, 0:1], FP8_MAX, ALU.mult, ALU.min))
                    ch.link(dve.tensor_scalar(qc, qc, -FP8_MAX, None, ALU.max))
                if t == 14:
                    ch.link(dve.tensor_scalar(qm.bitcast(I32), qc.bitcast(I32), 0x7F800000, None, ALU.bitwise_and))
                    ch.link(dve.tensor_scalar(qm, qm, 2.0 ** -6, 1.5 * 2.0 ** 20, ALU.max, ALU.mult))
                if t == 15:
                    ch.link(dve.tensor_tensor(qc, qc, qm, ALU.add))
                    dve.tensor_tensor(xq, qc, qm, ALU.subtract).then_inc(f_dve, 1)
                if t == 17:
                    dve.wait_ge(f_pe, F + 8)
                    dve.wait_ge(f_pool, FPOOL * g + 2)
                    ch.link(dve.tensor_tensor(flat(res[:]), GF[:], flat(xtok[:]), ALU.add))
                    norm_stats(ch, varf_ready)
                if t == 21:
                    norm_apply(rstdf_ready, 2 * g + 2, x2n).then_inc(f_dve, 1)
                if t in (26, 27, 28, 29, 30):
                    for db in range(DB):
                        k = t - 26 - db
                        if not 0 <= k < TAPS:
                            continue
                        if k == 0:
                            dve.wait_ge(f_act, A + 3 + db)
                        src = xpad[:, db, :, k:k + SEQ]
                        dst = cacc[:, db, :].rearrange("p (b t) -> p b t", b=NB)
                        w = convw[:, db * TAPS + k:db * TAPS + k + 1]
                        if k == 0:
                            last = dve.tensor_scalar(dst, src, w, convb[:, db:db + 1], ALU.mult, ALU.add)
                        else:
                            last = dve.scalar_tensor_tensor(dst, src, w, dst, ALU.mult, ALU.add)
                    if t < 30:
                        ch.link(last)
                    else:
                        last.then_inc(f_dve, 1)
                if t == 38:
                    dve.wait_ge(f_act, A + 10)
                    dve.scalar_tensor_tensor(cacc[:], pre[:], -1.0, pre[:], ALU.mult, ALU.min).then_inc(f_dve, 1)

            def commit(f):
                ch = Chain(dve, c_commit, f, CCOMMIT)
                dve.wait_ge(f_act, FACT * (f + 1))
                ch.link(dve.scalar_tensor_tensor(dlt[:], pre[:], 0.0, cacc[:], ALU.max, ALU.add))
                dve.tensor_tensor(dx[:], dlt[:], xn[:], ALU.mult)
                dve.tensor_copy(xc[:], xn[:])
                dve.tensor_copy(sz[:], szn[:]).then_inc(committed, 1)
                ch.done()

            def phase(part, a, f, s_, nxt=None):
                ch = Chain(dve, c_front, f, CFRONT) if f is not None else None
                if part == 1 and f is not None:
                    ch.n = CSPLIT
                bg = back_of(s_) if part == 0 else None
                chb = Chain(dve, c_back, bg, CBACK) if bg is not None else None
                for t, k, n in subslots(part, a, f, s_):
                    if a is not None and k < 8:
                        head_max(a, k, n)
                    if s_ is not None and k < 8:
                        (scan_half, gate_half)[n % 2](s_, k, n // 2)
                    if f is not None:
                        front(f, t, ch)
                    if a is not None and n == 3 and k < 8:
                        max_rows(a, k)
                    if bg is not None:
                        back(bg, t, Y[1] if a is not None else M[1], chb, s_)
                    if nxt is not None and t - JOBS in (1, 3):
                        attend_split(nxt, (t - JOBS) // 2)
                if chb is not None:
                    chb.done()
                if ch is not None and part == 0:
                    assert ch.n == CSPLIT, ch.n
                if ch is not None and part == 1:
                    ch.done()

            def between(a, g, f):
                if g is not None:
                    dve.wait_ge(y_mm, 8 * (g + 1))
                    for db in range(DB):
                        last = dve.scalar_tensor_tensor(yg[:, db, :], xc[:, db, :], dpar[:, db:db + 1], Y[db][:],
                                                        ALU.mult, ALU.add)
                    last.then_inc(y_in, 1)
                    dve.wait_ge(y_in, g + 1)
                    dve.tensor_tensor(yg, yg, sz[:], ALU.mult).then_inc(b_dve, 1)
                if f is not None:
                    commit(f)
                    if g is None:
                        dve.tensor_copy(x2[:], x2n[:])
                if is_first(a):
                    attend_split(a, 0)
                    attend_split(a, 1)
                if a is not None:
                    attend_v(a)
                if is_first(a):
                    prepare_rest()
                if g is not None and f is None:
                    ch = Chain(dve, c_back, g, CBACK)
                    for t in range(STEPS_B):
                        back(g, t, M[1], ch, None)
                    ch.done()

            def back(g, t, W, ch, f):
                if t == 1:
                    dve.wait_ge(b_pe, BPE * g + 1)
                    ch.link(dve.tensor_tensor(res[:].rearrange("p t c -> p (t c)"), W[:],
                                              x2[:].rearrange("p t c -> p (t c)"), ALU.add))
                    norm_stats(ch, varb_ready)
                    if f is not None:
                        dve.tensor_copy(x2[:], x2n[:])
                if t == 3:
                    norm_apply(rstdb_ready, g + 1, x3).then_inc(b_dve, 1)
                top, total, prob, kmax, pos, first, kept, slot = (r4[:, n, :] for n in range(8))
                wide = lambda a: a.unsqueeze(2).to_broadcast([P, TT, EXPERTS])
                if t == 5:
                    dve.wait_ge(b_pe, BPE * g + 3)
                    ch.link(dve.tensor_copy(lg[:].rearrange("p t e -> p (t e)"), W[:, 0:TT * EXPERTS]))
                    ch.link(dve.tensor_reduce(top, lg[:], AX, ALU.max))
                    dve.tensor_tensor(lg[:], lg[:], wide(top), ALU.subtract).then_inc(b_dve, 1)
                if t == 7:
                    dve.wait_ge(b_dve, BDVE * g + 3)
                    ch.link(dve.scalar_tensor_tensor(oh[:], lg[:], 0.0, key8[:], ALU.is_ge, ALU.mult))
                    ch.link(dve.tensor_reduce(kmax, oh[:], AX, ALU.max))
                    dve.tensor_tensor(oh[:], key8[:], wide(kmax), ALU.is_equal).then_inc(b_dve, 1)
                if t == 8:
                    dve.wait_ge(b_act, BACT * g + 2)
                    ch.link(dve.tensor_reduce(total, lge[:], AX, ALU.add))
                    ch.link(dve.reciprocal(prob, total))
                    dve.tensor_scalar(first, kmax, -float(CAP), float(CAP * EXPERTS), ALU.mult, ALU.add)
                    dve.wait_ge(b_pe, BPE * g + 4)
                    ch.link(dve.tensor_tensor(lge[:], W[:, 0:TT * EXPERTS].rearrange("p (t e) -> p t e", t=TT),
                                              carry[:].unsqueeze(1).to_broadcast([P, TT, EXPERTS]), ALU.add))
                    ch.link(dve.tensor_tensor(lge[:], lge[:], oh[:], ALU.mult))
                    dve.tensor_tensor(carry[:], carry[:], W[:, 32:32 + EXPERTS], ALU.add)
                    ch.link(dve.tensor_reduce(pos, lge[:], AX, ALU.add))
                    ch.link(dve.tensor_scalar(kept, pos, float(CAP), None, ALU.is_le))
                    ch.link(dve.tensor_tensor(gate[:, bass.ds(g * TT, TT)], prob, kept, ALU.mult))
                    ch.link(dve.tensor_scalar(slot, pos, float(CAP), -1.0, ALU.min, ALU.add))
                    ch.link(dve.tensor_tensor(slot, slot, first, ALU.add))
                    dve.tensor_copy(gidx[:, bass.ds(g * TT, TT)], slot)
                    ch.link(dve.tensor_tensor(pos, slot, dump[:], ALU.subtract))
                    ch.link(dve.tensor_tensor(pos, pos, kept, ALU.mult))
                    ch.link(dve.tensor_tensor(pos, pos, dump[:], ALU.add))
                    ch.link(dve.tensor_scalar(dump[:], dump[:], float(T), None, ALU.add))
                    dve.tensor_copy(sidx[:], pos).then_inc(b_dve, 1)

            stages(dve, phase, between)

            for e in range(EXPERTS):
                w = e % 2
                dve.wait_ge(we_in[w], 48 * (e // 2 + 1))
                dve.wait_ge(e_pe, down_count(e))
                if e >= 2:
                    dve.wait_ge(eo_out[w], 16 * (e // 2))
                dve.tensor_tensor(ye[w], Y[w][:, 0:CAP].rearrange("p (t c) -> p t c", c=P),
                                  b2s[w].unsqueeze(1).to_broadcast([P, ST, P]), ALU.add).then_inc(e_dve, 1)
            for g in range(GROUPS):
                ch = Chain(dve, c_back, 0, CBACK * GROUPS + 4 * (g + 1))
                ch.n = CBACK * GROUPS + 4 * g
                mine = x3all[:, g * TT:(g + 1) * TT, :]
                got = yall[:, g * TT:(g + 1) * TT, :]
                dve.wait_ge(gathered[g], 16 * TT)
                dve.wait_ge(b_act, BACT * GROUPS)
                ch.link(dve.tensor_tensor(got, got, gate[:, g * TT:(g + 1) * TT].unsqueeze(2)
                                          .to_broadcast([P, TT, P]), ALU.mult))
                ch.link(dve.tensor_tensor(res[:], got, mine, ALU.add))
                norm_stats(ch, varb_ready)
                norm_apply(rstdb_ready, GROUPS + g + 1, mine).then_inc(z_dve, 1)
                ch.done()

        @block.gpsimd
        def _(pool):
            pool.memset(zeros[:], 0.0).then_inc(consts, 1)
            pool.memset(ident[:], 0.0).then_inc(consts, 1)
            pool.memset(ones[:], 1.0).then_inc(consts, 1)
            pool.memset(mhalf[:], -0.5).then_inc(consts, 1)
            pool.iota(key8i[:], pattern=[[0, TT], [-1, EXPERTS]], base=EXPERTS, channel_multiplier=0
                      ).then_inc(consts, 1)
            pool.iota(dumpi[:], pattern=[[P, TT]], base=SLOTS, channel_multiplier=1).then_inc(consts, 1)
            pool.wait_ge(consts, 6)
            pool.affine_select(out=ident[:], in_=ident[:], compare_op=ALU.not_equal, fill=1.0, base=0,
                               pattern=[[-1, P]], channel_multiplier=1).then_inc(consts, 1)
            pool.affine_select(out=tri[:], in_=ones[:], compare_op=ALU.is_ge, fill=0.0, base=0,
                               pattern=[[1, P]], channel_multiplier=-1).then_inc(consts, 1)
            assert CONSTS == 8

            def power(ready, signal, count):
                pool.wait_ge(ready, count)
                pool.tensor_tensor(rstd[:], vpe[:], mhalf[:], ALU.pow).then_inc(signal, 1)

            def increments(g, st, half):
                c, db, at = st // DB, st % DB, slice(2 * half, 2 * half + 2)
                if half == 0:
                    if st == 0:
                        pool.wait_ge(committed, g + 1)
                    pool.wait_ge(b_in[c % 2], 16 * (2 * g + c // 2 + 1))
                    if st == 2:
                        wait(pool, b_pe, BPE * (g - 1) + 1)
                    if st >= 3:
                        pool.wait_ge(y_mm, 8 * g + st - 2)
                pool.tensor_tensor(u[st % 3][:, at, :], brep[c % 2][:, at, :],
                                   dx[:, db, :].unsqueeze(1).to_broadcast([P, 2, T]), ALU.mult).then_inc(u_ready, 1)

            def forget(g, st):
                wait_apart(pool, da_ready, 8 * g + st + 1)
                pool.memset(da[st % 2][:].rearrange("p n (b t) -> p n b t", b=NB)[:, :, :, 0:1], 0.0
                            ).then_inc(u_ready, 1)

            def fold(g, st):
                pool.wait_ge(h_ready, 2 * (8 * g + st + 1))
                ub = u[st % 3]
                pool.tensor_tensor(ub[:, 0:2, :], ub[:, 0:2, :], ub[:, 2:4, :], ALU.add).then_inc(a_ready, 1)

            def front(g, t):
                if t == 3:
                    pool.wait_ge(x_in, 16 * (g + 1))
                    pool.tensor_tensor(xtok[:], xtok[:], bproj_row.unsqueeze(1).to_broadcast([P, TT, P]), ALU.add
                                       ).then_inc(f_pool, 1)
                if t == 8:
                    power(varf_ready, rstdf_ready, 2 * g + 1)
                if t == 13:
                    pool.wait_ge(f_dve, FDVE * g + 5)
                    pool.tensor_tensor(xtok[:], x1[:], bff_row.unsqueeze(1).to_broadcast([P, TT, P]), ALU.add
                                       ).then_inc(f_pool, 1)
                if t == 18:
                    power(varf_ready, rstdf_ready, 2 * g + 2)

            def scatter(g):
                wait_apart(pool, b_dve, BDVE * (g + 1))
                pool.wait_ge(zeroed, 16 * (SLOTS // P))
                for t in range(TT):
                    pool.indirect_dma_start(buf, bass.IndirectOffsetOnAxis(ap=sidx[:, t:t + 1], axis=0),
                                            x3[:, t, :], None).then_inc(scattered, 16)

            def phase(part, a, f, s_, nxt=None):
                bg = back_of(s_) if part == 0 else None
                if s_ is not None and part == 0:
                    increments(s_, 0, 0)
                    increments(s_, 0, 1)
                    forget(s_, 0)
                for t, k, n in subslots(part, a, f, s_):
                    if f is not None:
                        front(f, t)
                    if bg is not None and t == 2:
                        power(varb_ready, rstdb_ready, bg + 1)
                    if s_ is not None:
                        if n == 0 and 1 <= k <= 8 and a is not None:
                            fold(s_, k - 1)
                        if n in (1, 2) and k < 7:
                            increments(s_, k + 1, n - 1)
                        if n == 3 and k < 7:
                            forget(s_, k + 1)
                    if bg is not None and t == 9:
                        scatter(bg)
                    if bg is not None and t == SPLIT - 1:
                        pool.wait_ge(scattered, 16 * TT * (bg + 1))

            def between(a, g, f):
                if g is not None and f is None:
                    power(varb_ready, rstdb_ready, g + 1)
                    scatter(g)

            pool.wait_ge(w_in, 16 * LOADS)
            stages(pool, phase, between)

            for e in range(EXPERTS):
                pool.wait_ge(e_dve, e + 1)
                pool.dma_start(eo[e * CAP:(e + 1) * CAP, :].rearrange("(t p) c -> p t c", p=P), ye[e % 2]
                               ).then_inc(eo_out[e % 2], 16)
            pool.wait_ge(eo_out[0], 16 * (EXPERTS // 2))
            pool.wait_ge(eo_out[1], 16 * (EXPERTS // 2))
            for g in range(GROUPS + 1):
                if g < GROUPS:
                    for t in range(g * TT, (g + 1) * TT):
                        pool.indirect_dma_start(yall[:, t, :], None, eo,
                                                bass.IndirectOffsetOnAxis(ap=gidx[:, t:t + 1], axis=0)
                                                ).then_inc(gathered[g], 16)
                if g >= 1:
                    power(varb_ready, rstdb_ready, GROUPS + g)


def kernel(**inputs):
    import numpy as np
    import concourse.bacc as bacc
    from concourse.bass_utils import run_bass_kernel_spmd as run

    a = {k: np.asarray(v) for k, v in inputs.items()}
    x = a["L0_attn_x"]
    B, S, C = x.shape
    flat = x.reshape(B * S, C)
    by_block = lambda v: v.reshape(DB, P, -1).transpose(1, 0, 2).reshape(P, -1)
    bq = a["L0_attn_b_qkv"]
    arrays = {
        "xT": flat.T, "x": flat,
        "wqkv": a["L0_attn_W_qkv"], "abqkv": np.concatenate([a["L0_attn_A_qkv"].T, a["L0_attn_B_qkv"]], 1),
        "wproj": a["L0_attn_W_proj"], "abproj": np.concatenate([a["L0_attn_A_proj"].T, a["L0_attn_B_proj"]], 1),
        "rows": np.concatenate([bq[2 * C:], a["L0_attn_b_proj"], a["L0_ffn_bias"], a["L1_attn_w_dt"]]),
        "cols": np.concatenate([bq[0:C, None], bq[C:2 * C, None], by_block(a["L1_attn_conv_w"]),
                                by_block(a["L1_attn_conv_b"]), by_block(a["L1_attn_D_param"]),
                                by_block(a["L1_attn_b_dt"]), by_block(a["L1_attn_A_log"])], 1),
        "wfp8T": a["L0_ffn_weight_fp8"].T,
        "scales": np.concatenate([a["L0_ffn_input_scale"], a["L0_ffn_weight_scale"]]),
        "win": a["L1_attn_W_in"], "wx": a["L1_attn_W_xproj"], "wout": a["L1_attn_W_out"],
        "rwT": a["L1_ffn_router_w"].T, "w1": a["L1_ffn_w1"],
        "b1c": a["L1_ffn_b1"].reshape(EXPERTS, FB, P).transpose(2, 0, 1),
        "w2": a["L1_ffn_w2"], "b2": a["L1_ffn_b2"],
    }
    arrays = {"in_" + k: np.ascontiguousarray(v) for k, v in arrays.items()}
    nc = bacc.Bacc("TRN2", target_bir_lowering=False, num_devices=1)
    args = [nc.dram_tensor(k, v.shape, F32, kind="ExternalInput").ap() for k, v in arrays.items()]
    N = B * S
    slots = EXPERTS * -(-3 * N // (2 * EXPERTS))
    buf = nc.dram_tensor("slots_in", (slots + N, C), F32, kind="Internal").ap()
    eo = nc.dram_tensor("slots_out", (slots, C), F32, kind="Internal").ap()
    parts = [nc.dram_tensor(f"parts{n}", (HEADS, len(QPARTS), HD, T), BF16, kind="Internal").ap() for n in range(2)]
    bcd = nc.dram_tensor("b_and_c", (N // T, 2 * STATES, T), F32, kind="Internal").ap()
    out = nc.dram_tensor("out_0", (N, C), F32, kind="ExternalOutput").ap()
    layers(nc, *args, buf, eo, parts, bcd, out)
    r = run(nc, [arrays], core_ids=[0])
    return r.results[0]["out_0"].reshape(B, S, C)
```

```python
from contextlib import ExitStack

import concourse.bass as bass
from concourse import mybir

F32 = mybir.dt.float32
BF16 = mybir.dt.bfloat16
I32 = mybir.dt.int32
U32 = mybir.dt.uint32
ALU = mybir.AluOpType
ACT = mybir.ActivationFunctionType
AX = mybir.AxisListType.X

P = 128
EPS = 1e-5
HEADS, HD = 16, 8
PAIRS = HEADS // 2
T = 512
TT = T // P
SEQ = 256
NB = T // SEQ
FP8_MAX = 448.0
STATES = 16
TAPS = 4
DB = 2
NC = 4
CHUNKS = STATES // NC
EXPERTS = 8
FF = 512
FB = FF // P
QPARTS = (0, 1, 2, 0, 1, 0)
KPARTS = (0, 0, 0, 1, 1, 2)
VW = 32
JOBS = HEADS * 2
LAG = 6
LAG_V = LAG + 2
SLOTS_A = 10
SLOTS_F = 10
SLOTS_S = 9
SPLIT = JOBS - 4
T_SILU = 31
TAIL = 38
STEPS_B = 12
CONSTS = 9
CFRONT, CSPLIT, CCOMMIT, CBACK = 17, 17, 1, 19
STACK = len(QPARTS) * HD


class Chain:

    def __init__(self, eng, sem, stage, per):
        self.eng, self.sem, self.base, self.per, self.n = eng, sem, stage * per, per, 0

    def link(self, ins):
        self.n += 1
        ins.then_inc(self.sem, 1)
        self.eng.wait_ge(self.sem, self.base + self.n)

    def done(self):
        assert self.n == self.per, (self.n, self.per)


def layers(nc, xT_in_d, x_in_d, wqkv_in, aqkvT_in, wproj_in, aprojT_in, rows_in, cols_in, wfp8T_in, scales_in,
           win_in, wx_in, wout_in, rwT_in, w1_in, b1c_in, w2_in, b2_in, buf, y, parts, bcd, out):
    N = x_in_d.shape[0]
    GROUPS = N // T
    TILES = N // P
    CAP = -(-3 * N // (2 * EXPERTS))
    SLOTS = EXPERTS * CAP
    ST = CAP // P
    assert CAP % P == 0

    with ExitStack() as ctx:
        def sb(name, shape, dt=F32):
            return ctx.enter_context(nc.sbuf_tensor(name, shape, dt))

        def psum(name, shape=(P, 512), dt=F32):
            return ctx.enter_context(nc.psum_tensor(name, list(shape), dt))

        def sem(name):
            return ctx.enter_context(nc.semaphore(name))

        ident = sb("ident", [P, P])
        tri = sb("tri", [P, P], BF16)
        ones = sb("ones", [P, P], BF16)
        wqkv = sb("wqkv", [P, 384])
        wproj = sb("wproj", [P, P])
        aq = sb("aq", [8, P])
        bq = sb("bq", [8, 384])
        ap_ = sb("ap_", [8, P])
        bp = sb("bp", [8, P])
        rows = sb("rows", [P, 3 * P + 2 * P])
        cols = sb("cols", [P, 2 + DB * (TAPS + 3 + STATES)])
        wf = sb("wf", [P, P])
        scales = sb("scales", [P, 2])
        rscale = sb("rscale", [P, 1])
        win = sb("win", [P, 4 * P])
        wx = sb("wx", [P, DB, 33])
        wd = sb("wd", [P, DB, DB * P])
        wout = sb("wout", [P, DB, P])
        rwT = sb("rwT", [P, EXPERTS])
        bqs = sb("bqs", [P, 1])
        aneg = sb("aneg", [P, DB, STATES])
        key8 = sb("key8", [P, TT, EXPERTS])
        key8i = sb("key8i", [P, TT, EXPERTS], I32)
        dump = sb("dump", [P, TT])
        dumpi = sb("dumpi", [P, TT], I32)
        spare = sb("spare", [P, SLOTS // P])
        sparei = sb("sparei", [P, SLOTS // P], I32)
        mhalf = sb("mhalf", [P, TT])
        carry = sb("carry", [P, EXPERTS])
        zeros = sb("zeros", [P, P + 1])

        NCOL = 0

        def col(n):
            nonlocal NCOL
            a = cols[:, NCOL:NCOL + n]
            NCOL += n
            return a

        bqc, bkc = col(1), col(1)
        convw = col(DB * TAPS)
        convb, dpar, bdt = col(DB), col(DB), col(DB)
        alog = col(DB * STATES)
        bv_row = rows[:, 0:P]
        bproj_row = rows[:, P:2 * P]
        bff_row = rows[:, 2 * P:3 * P]
        wdt_row = rows[:, 3 * P:5 * P]

        xT = sb("xT", [P, T])
        qparts = sb("qparts", [P, 2, 3, T], BF16)
        qs = sb("qs", [P, NB, PAIRS, SEQ], BF16)
        ks = sb("ks", [P, PAIRS, T], BF16)
        vaug = sb("vaug", [P, TT, HEADS, VW])
        mx = [sb(f"mx{n}", [P, 32], BF16) for n in range(2)]
        mrow = [sb(f"mrow{n}", [32, P], BF16) for n in range(2)]
        probs = sb("probs", [P, 4, 2, SEQ])
        qf = sb("qf", [P, 2, T])
        oq = sb("oq", [P, 4, T])
        xtok = sb("xtok", [P, TT, P])
        rden = sb("rden", [P, TT, HEADS])
        otok = sb("otok", [P, TT, P])
        oT = sb("oT", [P, T])
        x1 = sb("x1", [P, TT, P])
        x2n = sb("x2n", [P, TT, P])
        norms = [[sb(f"{what}{n}", [P, TT] + rest) for what, rest in
                  (("st6", [6]), ("mv", [2]), ("vpe", []), ("negmean", []), ("rstd", []), ("shift", []))]
                 for n in range(2)]
        pre = sb("pre", [P, DB, T])
        qc, qm = pre[:, 0, :], pre[:, 1, :]
        x2T = sb("x2T", [P, T])
        xq = x2T[:]
        xpad = sb("xpad", [P, DB, NB, SEQ + TAPS - 1])
        cacc = sb("cacc", [P, DB, T])
        xn = sb("xn", [P, DB, T])
        szn = sb("szn", [P, DB, T])
        bcf = sb("bcf", [2 * STATES, T])
        x2 = sb("x2", [P, TT, P])
        xc = sb("xc", [P, DB, T])
        sz = sb("sz", [P, DB, T])
        dlt = sb("dlt", [P, DB, T])
        dx = sb("dx", [P, DB, T])
        brep = [sb(f"brep{n}", [P, NC, T]) for n in range(2)]
        crep = [sb(f"crep{n}", [P, NC, T]) for n in range(2)]
        da = [sb(f"da{n}", [P, NC, T]) for n in range(2)]
        u = [sb(f"u{n}", [P, NC, T]) for n in range(3)]
        yg = u[2][:, 0:DB, :]
        x3 = sb("x3", [P, TT, P + 1])
        res4 = [brep[1][:, n, :].rearrange("p (t c) -> p t c", c=P) for n in range(2)]
        x3T = x2T
        x3all = sb("x3all", [P, TILES, P])
        lg = sb("lg", [P, TT, EXPERTS])
        lge = sb("lge", [P, TT, EXPERTS])
        oh = sb("oh", [P, TT, EXPERTS], BF16)
        r4 = sb("r4", [P, 8, TT])
        sidx = sb("sidx", [P, TT], U32)
        mark = [sb(f"mark{n}", [P, ST]) for n in range(2)]
        eidx = [sb(f"eidx{n}", [P, ST], U32) for n in range(2)]
        gate = sb("gate", [P, TILES])

        w1s = [da[0][:, n, :] for n in range(2)]
        w2s = [da[0][:, 2 + n, :].rearrange("p (f d) -> p f d", d=P) for n in range(2)]
        b2s = [da[1][:, 0, n * P:(n + 1) * P] for n in range(2)]
        xe = [da[1][:, 1 + n, 0:ST * (P + 1)].rearrange("p (t c) -> p t c", c=P + 1) for n in range(2)]
        xeT = [da[1][:, 3, 0:CAP], u[0][:, 0, 0:CAP]]
        hT = [u[0][:, 1, 0:CAP], u[0][:, 2, 0:CAP], u[0][:, 3, 0:CAP], u[1][:, 0, 0:CAP]]
        ye = [u[1][:, 1 + n, 0:CAP].rearrange("p (t c) -> p t c", c=P) for n in range(2)]
        b1c = sb("b1c", [P, EXPERTS, FB])
        yall = brep[0][:].rearrange("p n t -> p (n t)").rearrange("p (t c) -> p t c", c=P)

        E = [psum("E0"), psum("E1")]
        M = [psum("M0"), psum("M1")]
        V = psum("V")
        GF = psum("GF")
        Y = [psum("Y0"), psum("Y1")]

        wa_in = sem("wa_in")
        w_in = sem("w_in")
        zeroed = sem("zeroed")
        consts = sem("consts")
        prep_pe, prep_act, prep_dve = sem("prep_pe"), sem("prep_act"), sem("prep_dve")
        xT_in, x_in = sem("xT_in"), sem("x_in")
        qkv_mm = sem("qkv_mm")
        parts_ready = sem("parts_ready")
        vaug_ready = sem("vaug_ready")
        q_read, q_split = sem("q_read"), sem("q_split")
        parts_out = sem("parts_out")
        stack_in = [sem("stack_in0"), sem("stack_in1")]
        max_mm, max_read = sem("max_mm"), sem("max_read")
        mrow_ready = sem("mrow_ready")
        mrow_in = [sem("mrow_in0"), sem("mrow_in1")]
        qk_mm, exp_done, pv_mm = sem("qk_mm"), sem("exp_done"), sem("pv_mm")
        ov_read = sem("ov_read")
        f_pe, f_act, f_dve, f_pool = sem("f_pe"), sem("f_act"), sem("f_dve"), sem("f_pool")
        FPE, FACT, FDVE, FPOOL = 16, 14, 7, 2
        varf_ready, rstdf_ready = sem("varf_ready"), sem("rstdf_ready")
        varb_ready, rstdb_ready = sem("varb_ready"), sem("rstdb_ready")
        powf, powb = sem("powf"), sem("powb")
        committed = sem("committed")
        bc_out = sem("bc_out")
        b_in = [sem("b_in0"), sem("b_in1")]
        c_in = [sem("c_in0"), sem("c_in1")]
        da_ready = sem("da_ready")
        u_ready = sem("u_ready")
        a_ready = sem("a_ready")
        h_ready = sem("h_ready")
        scanned = sem("scanned")
        y_mm = sem("y_mm")
        y_in = sem("y_in")
        b_pe, b_act, b_dve = sem("b_pe"), sem("b_act"), sem("b_dve")
        BPE, BACT, BDVE = 4, 4, 4
        scattered = sem("scattered")
        c_front, c_back, c_commit, c_exp = sem("c_front"), sem("c_back"), sem("c_commit"), sem("c_exp")
        b1_in = sem("b1_in")
        passed = sem("passed")
        we_in = [sem("we_in0"), sem("we_in1")]
        tok_in = [sem("tok_in0"), sem("tok_in1")]
        rows_out = [sem("rows_out0"), sem("rows_out1")]
        e_pe, e_act, e_dve, e_idx = sem("e_pe"), sem("e_act"), sem("e_dve"), sem("e_idx")
        EPE, EACT = 2 + FB, 1 + FB
        y_loaded = [sem(f"y_loaded{g}") for g in range(GROUPS)]
        z_act = sem("z_act")
        out_done = sem("out_done")

        block = ctx.enter_context(nc.Block())
        LOADS_A, LOADS = 5, 9
        PREP_DVE = 18

        def wait(eng, signal, count):
            if not isinstance(count, int) or count > 0:
                eng.wait_ge(signal, count)

        def wait_apart(eng, signal, count):
            wait(eng, signal, count)
            eng.sem_inc(passed, 1)

        def is_first(g):
            return isinstance(g, int) and g == 0

        def stages(eng, phase, between):
            between(0, None, None)
            phase(0, 0, None, None)
            phase(1, 0, None, None, 1)
            between(1, None, None)
            phase(0, 1, 0, None)
            phase(1, 1, 0, None, 2)
            between(2, None, 0)
            phase(0, 2, 1, 0)
            with eng.Fori(1, GROUPS - 2) as g:
                phase(1, g + 1, g, g - 1, g + 2)
                between(g + 2, g - 1, g)
                phase(0, g + 2, g + 1, g)
            phase(1, GROUPS - 1, GROUPS - 2, GROUPS - 3)
            between(None, GROUPS - 3, GROUPS - 2)
            phase(0, None, GROUPS - 1, GROUPS - 2)
            phase(1, None, GROUPS - 1, GROUPS - 2)
            between(None, GROUPS - 2, GROUPS - 1)
            phase(0, None, None, GROUPS - 1)
            phase(1, None, None, GROUPS - 1)
            between(None, GROUPS - 1, None)

        def back_of(s_):
            return None if s_ is None or is_first(s_) else s_ - 1

        def subslots(part, a, f, s_):
            n = max(SLOTS_A if a is not None else 0, SLOTS_F if f is not None else 0, SLOTS_S if s_ is not None else 0)
            return [(t, t // 4, t % 4) for t in (range(SPLIT) if part == 0 else range(SPLIT, 4 * n))]

        def up_count(e, f):
            return 1 + EPE * e + f + 1

        def turn_count(e):
            return 1 if e == 0 else 1 + EPE * (e - 1) + FB + 1

        def down_count(e):
            return 1 + EPE * e + FB + (2 if e + 1 < EXPERTS else 1)

        @block.sync
        def _(sp):
            def load(signal, *pairs):
                for dst, src in pairs:
                    sp.dma_start(dst, src).then_inc(signal, 16)

            load(wa_in, (wqkv[:], wqkv_in), (aq[:], aqkvT_in[:, 0:P]), (bq[:], aqkvT_in[:, P:]), (cols[:], cols_in),
                 (rows[:], rows_in.partition_broadcast(P)))

            def load_rest():
                load(w_in, (wproj[:], wproj_in), (ap_[:], aprojT_in[:, 0:P]), (bp[:], aprojT_in[:, P:]),
                     (wf[:], wfp8T_in), (scales[:], scales_in.partition_broadcast(P)), (win[:], win_in),
                     (wx[:], wx_in.rearrange("(b p) n -> p b n", p=P)),
                     (wout[:], wout_in.rearrange("(b p) n -> p b n", p=P)), (rwT[:], rwT_in))
                sp.wait_ge(consts, CONSTS)
                for dst, n in ((buf[0:SLOTS, :], SLOTS // P), (y[0:N, :], TILES)):
                    dst = dst.rearrange("(r p) c -> p r c", p=P)
                    sp.dma_start(dst, zeros[:, 0:dst.shape[2]].unsqueeze(1).to_broadcast([P, n, dst.shape[2]])
                                 ).then_inc(zeroed, 16)

            def load_states(s_, c, which):
                dst, signal = (brep, crep)[which][c % 2], (b_in, c_in)[which][c % 2]
                row = which * STATES + NC * c
                if c >= 2 and which == 0:
                    wait_apart(sp, u_ready, 3 * (8 * s_ + 2 * (c - 1)))
                if c >= 2 and which == 1:
                    wait_apart(sp, h_ready, 2 * (8 * s_ + 2 * (c - 1)))
                sp.dma_start(dst[:], bcd[bass.ds(s_, 1), row:row + NC, :].rearrange("o n t -> o (n t)")
                                 .to_broadcast([P, NC * T]).rearrange("p (n t) -> p n t", n=NC)).then_inc(signal, 16)

            def load_x(a):
                wait_apart(sp, qkv_mm, 3 * a)
                sp.dma_start(xT[:], xT_in_d[:, bass.ds(a * T, T)]).then_inc(xT_in, 16)

            def store_part(a, r):
                if r < 2:
                    sp.wait_ge(q_read, 4 * a + 3 + r)
                else:
                    sp.wait_ge(parts_ready, a + 1)
                for n, order in enumerate((QPARTS, KPARTS)):
                    for m, part in enumerate(order):
                        if part == r:
                            sp.dma_start(parts[n][:, m], qparts[:, n, r, :]).then_inc(parts_out, 16)

            def load_stacks(a):
                wait_apart(sp, parts_out, 16 * 2 * len(QPARTS) * (a + 1))
                wait_apart(sp, qk_mm, 32 * a)
                if is_first(a):
                    sp.wait_ge(prep_dve, 5)
                for i in range(2):
                    q_rows, k_rows = (parts[n].rearrange("(j i) n d t -> i (n d) j t", i=2)[i] for n in range(2))
                    for b in range(NB):
                        sp.dma_start(qs[64 * i:64 * i + STACK, b], q_rows[:, :, b * SEQ:(b + 1) * SEQ]
                                     ).then_inc(stack_in[i], 16)
                    sp.dma_start(ks[64 * i:64 * i + STACK], k_rows).then_inc(stack_in[i], 16)

            def between(a, g, f):
                if is_first(a):
                    load_x(a)
                    load_rest()
                    for r in range(3):
                        store_part(a, r)
                if f is not None:
                    wait_apart(sp, bc_out, 16 * (f + 1))
                    wait_apart(sp, h_ready, 2 * 8 * f)
                    load_states(f, 0, 0)
                if a is not None:
                    load_stacks(a)
                if f is not None:
                    load_states(f, 0, 1)
                    load_states(f, 1, 0)
                    load_states(f, 1, 1)

            def phase(part, a, f, s_, nxt=None):
                if f is not None and part == 0:
                    wait_apart(sp, committed, f)
                    sp.dma_start(xtok[:], x_in_d[bass.ds(f * T, T), :].rearrange("(t p) c -> p t c", p=P)
                                 ).then_inc(x_in, 16)
                if nxt is not None:
                    load_x(nxt)
                for t, k, n in subslots(part, a, f, s_):
                    if n == 3 and a is not None and k < 8:
                        q = k
                        b, j = q // 4, 2 * (q % 4)
                        sp.wait_ge(mrow_ready, 8 * a + q + 1)
                        for i in range(2):
                            dst = qs[64 * i + STACK:64 * i + STACK + 1, b, j:j + 2, :]
                            sp.dma_start(dst.rearrange("o j (a t) -> o (j a) t", a=2),
                                         mrow[q % 2][4 * i:4 * i + 4, :]).then_inc(mrow_in[q % 2], 16)
                    if n == 3 and s_ is not None and k in (1, 3):
                        load_states(s_, (k + 3) // 2, 0)
                        load_states(s_, (k + 3) // 2, 1)
                if nxt is not None:
                    store_part(nxt, 0)
                    store_part(nxt, 1)
                if f is not None and part == 1:
                    sp.wait_ge(f_act, FACT * f + 10)
                    sp.dma_start(bcd[bass.ds(f, 1), :, :].rearrange("o n t -> (o n) t"), bcf[:]).then_inc(bc_out, 16)
                if nxt is not None:
                    store_part(nxt, 2)

            stages(sp, phase, between)

            sp.wait_ge(y_mm, 8 * GROUPS)
            for e in range(EXPERTS):
                w = e % 2

                if e >= 2:
                    sp.wait_ge(e_pe, turn_count(e - 2))
                    sp.wait_ge(e_idx, e - 1)
                    sp.dma_start(xe[w], buf[e * CAP:(e + 1) * CAP, :].rearrange("(t p) c -> p t c", p=P)
                                 ).then_inc(tok_in[w], 16)
                    sp.wait_ge(e_pe, down_count(e - 2))
                    sp.wait_ge(e_dve, e - 1)
                sp.dma_start(w1s[w], w1_in[e]).then_inc(we_in[w], 16)
                sp.dma_start(w2s[w], w2_in[e].rearrange("(f p) d -> p f d", p=P)).then_inc(we_in[w], 16)
                sp.dma_start(b2s[w], b2_in[e].partition_broadcast(P)).then_inc(we_in[w], 16)
                if e == 1:
                    sp.wait_ge(scattered, 16 * TILES)
                    for w in range(2):
                        sp.dma_start(xe[w], buf[w * CAP:(w + 1) * CAP, :].rearrange("(t p) c -> p t c", p=P)
                                     ).then_inc(tok_in[w], 16)
            for w in range(2):
                sp.wait_ge(rows_out[w], 16 * ST * (EXPERTS // 2))
            for g in range(GROUPS):
                sp.dma_start(yall[:, g * TT:(g + 1) * TT, :], y[g * T:(g + 1) * T, :].rearrange("(t p) c -> p t c", p=P)
                             ).then_inc(y_loaded[g], 16)
            for g in range(GROUPS):
                sp.wait_ge(z_act, g + 1)
                sp.dma_start(out[g * T:(g + 1) * T, :].rearrange("(t p) c -> p t c", p=P),
                             x3all[:, g * TT:(g + 1) * TT, :]).then_inc(out_done, 16)
            sp.wait_ge(out_done, 16 * GROUPS)

        @block.tensor
        def _(pe):
            pe.wait_ge(wa_in, 16 * LOADS_A)
            pe.matmul(E[0][:, 0:384], aq[:], bq[:], start=True, stop=True).then_inc(prep_pe, 1)
            pe.wait_ge(prep_dve, 2)

            def turn(dst, src, n=TT):
                for t in range(n):
                    last = pe.transpose(dst[:, t * P:(t + 1) * P], src[:, t, :], ident[:])
                return last

            def attend_qk(a):
                pe.wait_ge(xT_in, 16 * (a + 1))
                wait(pe, max_read, 32 * a - 1)
                pe.matmul(M[0][:], wqkv[:, 0:P], xT[:], start=True, stop=True).then_inc(qkv_mm, 1)
                wait(pe, max_read, 32 * a)
                pe.matmul(M[1][:], wqkv[:, P:2 * P], xT[:], start=True, stop=True).then_inc(qkv_mm, 1)

            def attend_v(a):
                wait(pe, ov_read, 8 * a)
                for t in range(TT):
                    last = pe.matmul(V[:, t * P:(t + 1) * P], xT[:, t * P:(t + 1) * P], wqkv[:, 2 * P:],
                                     start=True, stop=True)
                last.then_inc(qkv_mm, 1)

            def max_head(a, q, n):
                b, j, i = q // 4, 2 * (q % 4) + n // 2, n % 2
                if q == 0 and n == 0:
                    wait(pe, q_read, 4 * a + 2)
                if q == 0 and n < 2:
                    pe.wait_ge(stack_in[n], 16 * 3 * (a + 1))
                wait(pe, max_read, 32 * a + 4 * q + n - 1)
                at = slice(64 * i, 64 * i + STACK)
                for t in range(2):
                    last = pe.matmul(M[n % 2][:, t * SEQ:(t + 1) * SEQ],
                                     qs[at, b, j, t * P:(t + 1) * P],
                                     ks[at, j, b * SEQ:(b + 1) * SEQ], start=True, stop=True)
                last.then_inc(max_mm, 1)

            def score_head(a, q, n):
                b, j, i = q // 4, 2 * (q % 4) + n // 2, n % 2
                h = 32 * a + 4 * q + n
                if n == 0:
                    pe.wait_ge(mrow_in[q % 2], 32 * (4 * a + q // 2 + 1))
                wait(pe, exp_done, h - 1)
                at = slice(64 * i, 64 * i + STACK + 1)
                for t in range(2):
                    last = pe.matmul(E[n % 2][:, t * SEQ:(t + 1) * SEQ],
                                     ks[at, j, b * SEQ + t * P:b * SEQ + (t + 1) * P],
                                     qs[at, b, j, :], start=True, stop=True)
                last.then_inc(qk_mm, 1)

            def value_head(a, q, n):
                b, h = q // 4, 4 * (q % 4) + n
                pe.wait_ge(exp_done, 32 * a + 4 * q + n + 1)
                if n == 0:
                    if q == 0:
                        pe.wait_ge(vaug_ready, a + 1)
                    wait(pe, ov_read, 8 * a + q)
                for kt in range(2):
                    last = pe.matmul(V[VW * n:VW * (n + 1), 0:SEQ], vaug[:, 2 * b + kt, h, :], probs[:, n, kt, :],
                                     start=(kt == 0), stop=(kt == 1))
                last.then_inc(pv_mm, 1)

            def states_sum(g, st, n, count):
                c, db = st // DB, st % DB
                if count == NC and n % 2 == 0:
                    pe.wait_ge(h_ready, 2 * (8 * g + st) + n // 2 + 1)
                if count < NC and n == 0:
                    pe.wait_ge(a_ready, 8 * g + st + 1)
                    if st == 1:
                        wait(pe, b_dve, BDVE * (g - 1) + 4)
                last = pe.matmul(Y[db][:], ident[:], u[st % 3][:, n, :], start=(c == 0 and n == 0),
                                 stop=(c == CHUNKS - 1 and n == count - 1), skip_group_check=True)
                if n == count - 1:
                    last.then_inc(y_mm, 1)

            def front(g, t):
                F, A, D = FPE * g, FACT * g, FDVE * g
                if t < 4:
                    if t == 0:
                        wait(pe, ov_read, 8 * (g + 1))
                        wait(pe, f_act, A)
                    else:
                        pe.wait_ge(f_dve, D + t)
                    turn(GF, oq[:, :, t * P:(t + 1) * P]).then_inc(f_pe, 1)
                if t == 5:
                    pe.wait_ge(f_dve, D + 4)
                    turn(GF, otok).then_inc(f_pe, 1)
                if t == 7:
                    pe.wait_ge(f_act, A + 1)
                    pe.wait_ge(f_pool, FPOOL * g + 1)
                    product_and_rest(GF, oT, wproj, xtok).then_inc(f_pe, 1)
                if t == 11:
                    pe.wait_ge(f_act, A + 2)
                    turn(GF, x1).then_inc(f_pe, 1)
                if t == 15:
                    pe.wait_ge(f_dve, D + 5)
                    pe.wait_ge(f_pool, FPOOL * g + 2)
                    product_and_rest(GF, xq, wf, xtok).then_inc(f_pe, 1)
                if t == 19:
                    pe.wait_ge(f_act, A + 3)
                    turn(GF, x2n).then_inc(f_pe, 1)
                if t in (21, 23, 25, 27):
                    n = (t - 21) // 2
                    pe.wait_ge(f_act, A + 4 + n)
                    pe.matmul(GF[:], win[:, n * P:(n + 1) * P], x2T[:], start=True, stop=True
                              ).then_inc(f_pe, 1)
                if t == T_SILU + 1:
                    pe.wait_ge(f_act, A + 9)
                    for eb in range(DB):
                        last = pe.matmul(GF[0:32, :], wx[:, eb, 1:33], xn[:, eb, :], start=(eb == 0), stop=(eb == 1))
                    last.then_inc(f_pe, 1)
                if t in (T_SILU + 2, T_SILU + 4):
                    db = (t - T_SILU - 2) // 2
                    pe.wait_ge(f_act, A + 10 + db)
                    for eb in range(DB):
                        last = pe.matmul(GF[:], wd[:, eb, db * P:(db + 1) * P], xn[:, eb, :],
                                         start=(eb == 0), stop=(eb == 1))
                    last.then_inc(f_pe, 1)

            def product_and_rest(dst, xT_, w, rest):
                for m in range(TT):
                    pe.matmul(dst[:, m * P:(m + 1) * P], xT_[:, m * P:(m + 1) * P], w[:], start=True, stop=False)
                    last = pe.matmul(dst[:, m * P:(m + 1) * P], ident[:], rest[:, m, :], start=False, stop=True)
                return last

            def back(g, t, W):
                if t == 0:
                    pe.wait_ge(b_dve, BDVE * g + 1)
                    for m in range(TT):
                        for db in range(DB):
                            pe.matmul(W[:, m * P:(m + 1) * P], yg[:, db, m * P:(m + 1) * P], wout[:, db, :],
                                      start=(db == 0), stop=False)
                        last = pe.matmul(W[:, m * P:(m + 1) * P], ident[:], x2[:, m, :], start=False, stop=True)
                    last.then_inc(b_pe, 1)
                if t == 4:
                    pe.wait_ge(b_act, BACT * g + 1)
                    turn(W, x3[:, :, 0:P]).then_inc(b_pe, 1)
                if t == 5:
                    pe.wait_ge(b_act, BACT * g + 2)
                    for m in range(TT):
                        last = pe.matmul(W[:, m * 8:(m + 1) * 8], x3T[:, m * P:(m + 1) * P], rwT[:],
                                         start=True, stop=True)
                    last.then_inc(b_pe, 1)
                if t == 8:
                    pe.wait_ge(b_dve, BDVE * g + 3)
                    counts = W[:, 0:TT * EXPERTS].rearrange("p (t e) -> p t e", t=TT)
                    pe.matmul(counts, tri[:], oh[:], start=True, stop=False, skip_group_check=True)
                    for v in range(TT - 1):
                        pe.matmul(counts[:, v + 1:], ones[:], oh[:, v:v + 1, :].to_broadcast([P, TT - 1 - v, EXPERTS]),
                                  start=False, stop=(v == TT - 2), skip_group_check=True)
                    for m in range(TT):
                        last = pe.matmul(W[:, 32:40], ones[:], oh[:, m, :], start=(m == 0), stop=(m == TT - 1))
                    last.then_inc(b_pe, 1)

            def phase(part, a, f, s_, nxt=None):
                for t, k, n in subslots(part, a, f, s_):
                    if a is not None:
                        if t < JOBS:
                            max_head(a, t // 4, t % 4)
                        if 0 <= t - LAG < JOBS:
                            score_head(a, (t - LAG) // 4, (t - LAG) % 4)
                        if 0 <= t - LAG_V < JOBS:
                            value_head(a, (t - LAG_V) // 4, (t - LAG_V) % 4)
                    if s_ is not None:
                        if a is None and 2 <= t < 34:
                            states_sum(s_, (t - 2) // 4, (t - 2) % 4, NC)
                        if a is not None and 1 <= k <= 8 and n >= 2:
                            states_sum(s_, k - 1, n - 2, 2)
                    if f is not None:
                        front(f, t)
                    if back_of(s_) is not None:
                        back(back_of(s_), t, Y[1] if a is not None else M[1])
                    if nxt is not None and t == JOBS:
                        attend_qk(nxt)

            def between(a, g, f):
                if is_first(a):
                    attend_qk(a)
                if a is not None:
                    attend_v(a)
                if is_first(a):
                    pe.wait_ge(w_in, 16 * LOADS)
                    pe.matmul(GF[:, 0:P], ap_[:], bp[:], start=True, stop=True).then_inc(prep_pe, 1)
                    pe.wait_ge(consts, CONSTS)
                    pe.wait_ge(prep_dve, PREP_DVE)
                if g is not None and f is None:
                    for t in range(STEPS_B):
                        back(g, t, M[1])

            stages(pe, phase, between)

            def e_turn(e):
                pe.wait_ge(tok_in[e % 2], 16 * (e // 2 + 1))
                if e >= 2:
                    pe.wait_ge(e_act, EACT * (e - 2) + 1)
                turn((GF, M[1])[e % 2], xe[e % 2][:, :, 0:P], ST).then_inc(e_pe, 1)

            pe.wait_ge(b_dve, BDVE * GROUPS)
            e_turn(0)
            for e in range(EXPERTS):
                w = e % 2
                pe.wait_ge(we_in[w], 48 * (e // 2 + 1))
                pe.wait_ge(e_act, EACT * e + 1)
                for f, bank in enumerate((E[0], E[1], M[0], V)):
                    if e >= 1:
                        pe.wait_ge(e_act, EACT * (e - 1) + 2 + f)
                    pe.matmul(bank[:, 0:CAP], w1s[w][:, f * P:(f + 1) * P], xeT[w], start=True, stop=True
                              ).then_inc(e_pe, 1)
                if e + 1 < EXPERTS:
                    e_turn(e + 1)
                pe.wait_ge(e_act, EACT * e + 1 + FB)
                if e >= 2:
                    pe.wait_ge(e_dve, e - 1)
                for t in range(ST):
                    for f in range(FB):
                        last = pe.matmul(Y[w][:, t * P:(t + 1) * P], hT[f][:, t * P:(t + 1) * P], w2s[w][:, f, :],
                                         start=(f == 0), stop=(f == FB - 1))
                last.then_inc(e_pe, 1)

        @block.scalar
        def _(act):
            act.dma_start(b1c[:], b1c_in).then_inc(b1_in, 16)
            act.wait_ge(wa_in, 16 * LOADS_A)
            act.activation(aneg[:].rearrange("p b n -> p (b n)"), alog, ACT.Exp).then_inc(prep_act, 1)

            def attend_pre(a, step):
                if step == 0:
                    wait(act, parts_ready, a)
                    act.wait_ge(qkv_mm, 3 * a + 1)
                    act.activation(qf[:, 0, :], M[0][:], ACT.Identity, bias=bqs[:, 0:1], scale=HD ** -0.5
                                   ).then_inc(q_read, 1)
                    act.wait_ge(qkv_mm, 3 * a + 2)
                    act.activation(qf[:, 1, :], M[1][:], ACT.Identity, bias=bkc).then_inc(q_read, 1)
                if step == 1:
                    wait(act, parts_out, 16 * 2 * len(QPARTS) * a)
                    act.wait_ge(q_read, 4 * a + 2)
                    act.copy(qparts[:, :, 0, :], qf[:]).then_inc(q_read, 1)
                if step == 2:
                    act.wait_ge(q_split, a + 1)
                    act.copy(qparts[:, :, 1, :], qf[:]).then_inc(q_read, 1)

            def exp_head(a, q, n):
                h = 32 * a + 4 * q + n
                act.wait_ge(qk_mm, h + 1)
                wait(act, pv_mm, h - 3)
                act.activation(probs[:, n].rearrange("p k t -> p (k t)"), E[n % 2][:], ACT.Exp).then_inc(exp_done, 1)

            def read_values(a, q):
                act.wait_ge(pv_mm, 32 * a + 4 * q + 4)
                if q == 0:
                    wait(act, f_pe, FPE * (a - 1) + 4)
                b = q // 4
                act.copy(oq[:, q % 4, b * SEQ:(b + 1) * SEQ], V[:, 0:SEQ]).then_inc(ov_read, 1)

            def decay(g, st, n):
                c, db = st // DB, st % DB
                if st == 0 and n == 0:
                    act.wait_ge(c_commit, CCOMMIT * g + 1)
                if st >= 2 and n == 0:
                    act.wait_ge(scanned, 2 * (8 * g + st - 1))
                last = act.activation(da[st % 2][:, n, :], dlt[:, db, :], ACT.Exp,
                                      scale=aneg[:, db, NC * c + n:NC * c + n + 1])
                if n == NC - 1:
                    last.then_inc(da_ready, 1)

            def norm_apply(norm, signal, count, src, dst):
                act.wait_ge(signal, count)
                rstd, shift = norm[4], norm[5]
                for t in range(TT):
                    last = act.activation(dst[:, t, :], src[:, t, :], ACT.Identity, bias=shift[:, t:t + 1],
                                          scale=rstd[:, t:t + 1])
                return last

            def tiles(bank):
                return bank[:].rearrange("p (t c) -> p t c", c=P)

            def front(g, t):
                F = FPE * g
                if t == 5:
                    act.wait_ge(f_pe, F + 5)
                    act.copy(oT[:], GF[:]).then_inc(f_act, 1)
                if t == 10:
                    norm_apply(norms[0], rstdf_ready, 2 * g + 1, tiles(GF), x1).then_inc(f_act, 1)
                if t == 18:
                    norm_apply(norms[0], rstdf_ready, 2 * g + 2, tiles(GF), x2n).then_inc(f_act, 1)
                if t == 20:
                    act.wait_ge(f_pe, F + 9)
                    act.copy(x2T[:], GF[:]).then_inc(f_act, 1)
                if t in (22, 24):
                    db = (t - 22) // 2
                    act.wait_ge(f_pe, F + 10 + db)
                    act.copy(xpad[:, db, :, TAPS - 1:], GF[:].rearrange("p (b t) -> p b t", b=NB)
                             ).then_inc(f_act, 1)
                if t in (26, 28):
                    db = (t - 26) // 2
                    act.wait_ge(f_pe, F + 12 + db)
                    act.copy(szn[:, db, :], GF[:]).then_inc(f_act, 1)
                if t == T_SILU:
                    act.wait_ge(f_act, FACT * g + 8)
                    act.activation(szn[:], szn[:], ACT.Silu)
                    act.wait_ge(f_dve, FDVE * g + 6)
                    act.activation(xn[:], cacc[:], ACT.Silu).then_inc(f_act, 1)
                if t == T_SILU + 1:
                    act.wait_ge(f_pe, F + 14)
                    act.copy(bcf[:], GF[0:32, :]).then_inc(f_act, 1)
                if t in (T_SILU + 3, T_SILU + 5):
                    db = (t - T_SILU - 3) // 2
                    act.wait_ge(f_pe, F + 15 + db)
                    act.activation(pre[:, db, :], GF[:], ACT.Identity, bias=bdt[:, db:db + 1]).then_inc(f_act, 1)
                if t == T_SILU + 6:
                    act.wait_ge(f_dve, FDVE * g + 7)
                    act.activation(cacc[:], cacc[:], ACT.Exp).then_inc(f_act, 1)
                    act.wait_ge(f_act, FACT * g + 13)
                    act.activation(cacc[:], cacc[:], ACT.Ln, bias=1.0).then_inc(f_act, 1)

            def back(g, t, W):
                if t == 3:
                    norm_apply(norms[1], rstdb_ready, g + 1, tiles(W), x3[:, :, 0:P]).then_inc(b_act, 1)
                if t == 4:
                    act.wait_ge(b_pe, BPE * g + 2)
                    act.copy(x3T[:], W[:]).then_inc(b_act, 1)
                if t == 6:
                    act.wait_ge(b_dve, BDVE * g + 2)
                    act.activation(lge[:], lg[:], ACT.Exp).then_inc(b_act, 1)
                    act.copy(x3all[:, bass.ds(g * TT, TT), :], x3[:, :, 0:P]).then_inc(b_act, 1)

            def phase(part, a, f, s_, nxt=None):
                for t, k, n in subslots(part, a, f, s_):
                    if a is not None:
                        v = t - LAG_V - 4
                        if v >= 0 and v % 4 == 0:
                            read_values(a, v // 4)
                        if 0 <= t - LAG < JOBS:
                            exp_head(a, (t - LAG) // 4, (t - LAG) % 4)
                        if t == LAG_V + JOBS - 1:
                            read_values(a, JOBS // 4 - 1)
                    if s_ is not None:
                        if k < 7:
                            decay(s_, k + 1, n)
                    if f is not None:
                        front(f, t)
                    if back_of(s_) is not None:
                        back(back_of(s_), t, Y[1] if a is not None else M[1])
                    if nxt is not None and JOBS <= t < JOBS + 3:
                        attend_pre(nxt, t - JOBS)

            def between(a, g, f):
                if is_first(a):
                    for step in range(3):
                        attend_pre(a, step)
                if f is not None:
                    for n in range(NC):
                        decay(f, 0, n)
                if g is not None and f is None:
                    for t in range(STEPS_B):
                        back(g, t, M[1])

            stages(act, phase, between)

            act.wait_ge(b1_in, 16)
            for e in range(EXPERTS):
                act.wait_ge(e_pe, turn_count(e))
                act.copy(xeT[e % 2], (GF, M[1])[e % 2][:, 0:CAP]).then_inc(e_act, 1)
                for f, bank in enumerate((E[0], E[1], M[0], V)):
                    act.wait_ge(e_pe, up_count(e, f))
                    if e >= 1 and f == 0:
                        act.wait_ge(e_pe, down_count(e - 1))
                    act.activation(hT[f], bank[:, 0:CAP], ACT.Gelu, bias=b1c[:, e, f:f + 1]).then_inc(e_act, 1)
            for g in range(GROUPS):
                norm_apply(norms[g % 2], rstdb_ready, GROUPS + g + 1, res4[g % 2], x3all[:, g * TT:(g + 1) * TT, :]
                           ).then_inc(z_act, 1)

        @block.vector
        def _(dve):
            prep = Chain(dve, prep_dve, 0, PREP_DVE)
            dve.wait_ge(wa_in, 16 * LOADS_A)
            prep.link(dve.tensor_scalar(bqs[:], bqc, HD ** -0.5, None, ALU.mult))
            dve.wait_ge(prep_pe, 1)
            prep.link(dve.scalar_tensor_tensor(wqkv[:], E[0][:, 0:384], 2.0, wqkv[:], ALU.mult, ALU.add))
            prep.link(dve.memset(vaug[:], 0.0))
            prep.link(dve.memset(vaug[:, :, :, HD:HD + 1], 1.0))

            def prepare_rest():
                prep.link(dve.memset(ks[:], 1.0))
                for n in range(2):
                    prep.link(dve.memset(mx[n][:], 0.0))
                dve.wait_ge(w_in, 16 * LOADS)
                dve.wait_ge(consts, CONSTS)
                dve.wait_ge(prep_act, 1)
                prep.link(dve.tensor_scalar(aneg[:], aneg[:], -1.0, None, ALU.mult))
                for eb in range(DB):
                    prep.link(dve.tensor_scalar(wd[:, eb, :], wdt_row, wx[:, eb, 0:1], None, ALU.mult))
                prep.link(dve.tensor_scalar(wf[:], wf[:], scales[:, 0:1], scales[:, 1:2], ALU.mult, ALU.mult))
                prep.link(dve.reciprocal(rscale[:], scales[:, 0:1]))
                prep.link(dve.tensor_copy(key8[:], key8i[:]))
                prep.link(dve.tensor_copy(dump[:], dumpi[:]))
                prep.link(dve.tensor_copy(spare[:], sparei[:]))
                prep.link(dve.memset(carry[:], 0.0))
                prep.link(dve.memset(xpad[:], 0.0))
                dve.wait_ge(prep_pe, 2)
                prep.link(dve.scalar_tensor_tensor(wproj[:], GF[:, 0:P], 2.0, wproj[:], ALU.mult, ALU.add))
                prep.done()

            def norm_stats(norm, src, ch, ready):
                st6, mv, vpe, negmean = norm[:4]
                for t in range(TT):
                    last = dve.bn_stats(st6[:, t, :], src[:, t, :])
                ch.n += 1
                last.then_inc(ch.sem, 1)
                wait_apart(dve, ch.sem, ch.base + ch.n)
                for t in range(TT):
                    last = dve.bn_aggr(mv[:, t, :], st6[:, t, :])
                ch.link(last)
                dve.tensor_scalar(negmean[:], mv[:, :, 0], -1.0, None, ALU.mult)
                dve.tensor_scalar(vpe[:], mv[:, :, 1], EPS, None, ALU.add).then_inc(ready, 1)

            def tiles(bank):
                return bank[:].rearrange("p (t c) -> p t c", c=P)

            def attend_split(a, step):
                if step == 0:
                    dve.wait_ge(q_read, 4 * a + 3)
                    dve.tensor_tensor(qf[:], qf[:], qparts[:, :, 0, :], ALU.subtract).then_inc(q_split, 1)
                if step == 1:
                    dve.wait_ge(q_read, 4 * a + 4)
                    dve.wait_ge(q_split, a + 1)
                    dve.tensor_tensor(qparts[:, :, 2, :], qf[:], qparts[:, :, 1, :], ALU.subtract
                                      ).then_inc(parts_ready, 1)

            def attend_v(a):
                dve.wait_ge(qkv_mm, 3 * a + 3)
                dve.tensor_tensor(vaug[:, :, :, 0:HD], V[:].rearrange("p (t h d) -> p t h d", t=TT, d=HD),
                                  bv_row.rearrange("p (h d) -> p h d", d=HD).unsqueeze(1)
                                  .to_broadcast([P, TT, HEADS, HD]), ALU.add).then_inc(vaug_ready, 1)

            def head_max(a, q, n):
                dve.wait_ge(max_mm, 32 * a + 4 * q + n + 1)
                c = 4 * (n % 2) + 2 * (n // 2)
                dve.tensor_reduce(mx[q % 2][:, c:c + 2], M[n % 2][:].rearrange("p (t k) -> p t k", t=2), AX, ALU.max,
                                  negate=True).then_inc(max_read, 1)

            def max_rows(a, q):
                dve.wait_ge(max_read, 32 * a + 4 * q + 4)
                wait(dve, mrow_in[q % 2], 32 * (4 * a + q // 2))
                for m in range(P // 32):
                    at = slice(32 * m, 32 * (m + 1))
                    last = dve.transpose(mrow[q % 2][:, at], mx[q % 2][at, :])
                last.then_inc(mrow_ready, 1)

            def scan_half(g, st, half):
                at = slice(2 * half, 2 * half + 2)
                if half == 0 or st == 0:
                    dve.wait_ge(u_ready, 3 * (8 * g + st + 1) - (1 if st == 0 and half == 0 else 0))
                ub = u[st % 3][:, at, :].rearrange("p n t -> p (n t)")
                dve.tensor_tensor_scan(ub, da[st % 2][:, at, :].rearrange("p n t -> p (n t)"), ub, 0.0,
                                       ALU.mult, ALU.add).then_inc(scanned, 1)

            def gate_half(g, st, half):
                c, at = st // DB, slice(2 * half, 2 * half + 2)
                dve.wait_ge(scanned, 2 * (8 * g + st) + half + 1)
                if half == 0:
                    dve.wait_ge(c_in[c % 2], 16 * (2 * g + c // 2 + 1))
                dve.tensor_tensor(u[st % 3][:, at, :], u[st % 3][:, at, :], crep[c % 2][:, at, :], ALU.mult
                                  ).then_inc(h_ready, 1)

            def front(g, t, ch):
                F, A, D = FPE * g, FACT * g, FDVE * g
                if t < 4:
                    dve.wait_ge(f_pe, F + t + 1)
                    v = GF[:].rearrange("p (h w) -> p h w", w=VW)
                    ch.link(dve.reciprocal(rden[:, t, :], v[:, :, HD]))
                    dve.tensor_tensor(otok[:, t, :].rearrange("p (h d) -> p h d", d=HD), v[:, :, 0:HD],
                                      rden[:, t, :].unsqueeze(2).to_broadcast([P, HEADS, HD]), ALU.mult
                                      ).then_inc(f_dve, 1)
                if t == 8:
                    dve.wait_ge(f_pe, F + 6)
                    norm_stats(norms[0], tiles(GF), ch, varf_ready)
                if t == 12:
                    dve.wait_ge(f_pe, F + 7)
                    ch.link(dve.tensor_scalar(qc, GF[:], rscale[:, 0:1], FP8_MAX, ALU.mult, ALU.min))
                    ch.link(dve.tensor_scalar(qc, qc, -FP8_MAX, None, ALU.max))
                if t == 13:
                    ch.link(dve.tensor_scalar(qm.bitcast(I32), qc.bitcast(I32), 0x7F800000, None, ALU.bitwise_and))
                    ch.link(dve.tensor_scalar(qm, qm, 2.0 ** -6, 1.5 * 2.0 ** 20, ALU.max, ALU.mult))
                if t == 14:
                    ch.link(dve.tensor_tensor(qc, qc, qm, ALU.add))
                    dve.tensor_tensor(xq, qc, qm, ALU.subtract).then_inc(f_dve, 1)
                if t == 16:
                    dve.wait_ge(f_pe, F + 8)
                    norm_stats(norms[0], tiles(GF), ch, varf_ready)
                if 24 <= t < 24 + TAPS + 1:
                    for db in range(DB):
                        k = t - 24 - db
                        if not 0 <= k < TAPS:
                            continue
                        if k == 0:
                            dve.wait_ge(f_act, A + 5 + db)
                        src = xpad[:, db, :, k:k + SEQ]
                        dst = cacc[:, db, :].rearrange("p (b t) -> p b t", b=NB)
                        w = convw[:, db * TAPS + k:db * TAPS + k + 1]
                        if k == 0:
                            last = dve.tensor_scalar(dst, src, w, convb[:, db:db + 1], ALU.mult, ALU.add)
                        else:
                            last = dve.scalar_tensor_tensor(dst, src, w, dst, ALU.mult, ALU.add)
                    if t < 24 + TAPS:
                        ch.link(last)
                    else:
                        last.then_inc(f_dve, 1)
                if t == T_SILU + 5:
                    dve.wait_ge(f_act, A + 12)
                    dve.scalar_tensor_tensor(cacc[:], pre[:], -1.0, pre[:], ALU.mult, ALU.min).then_inc(f_dve, 1)

            def y_out(g):
                dve.wait_ge(y_mm, 8 * (g + 1))
                for db in range(DB):
                    last = dve.scalar_tensor_tensor(yg[:, db, :], xc[:, db, :], dpar[:, db:db + 1], Y[db][:],
                                                    ALU.mult, ALU.add)
                last.then_inc(y_in, 1)
                dve.wait_ge(y_in, g + 1)
                dve.tensor_tensor(yg, yg, sz[:], ALU.mult).then_inc(b_dve, 1)

            def commit(f):
                ch = Chain(dve, c_commit, f, CCOMMIT)
                dve.wait_ge(f_act, FACT * (f + 1))
                ch.link(dve.scalar_tensor_tensor(dlt[:], pre[:], 0.0, cacc[:], ALU.max, ALU.add))
                dve.tensor_tensor(dx[:], dlt[:], xn[:], ALU.mult).then_inc(committed, 1)
                dve.tensor_copy(xc[:], xn[:])
                dve.tensor_copy(sz[:], szn[:])
                ch.done()

            def phase(part, a, f, s_, nxt=None):
                ch = Chain(dve, c_front, f, CFRONT) if f is not None else None
                if part == 1 and f is not None:
                    ch.n = CSPLIT
                bg = back_of(s_) if part == 0 else None
                chb = Chain(dve, c_back, bg, CBACK) if bg is not None else None
                for t, k, n in subslots(part, a, f, s_):
                    if s_ is not None and k < 8:
                        (scan_half, gate_half)[n % 2](s_, k, n // 2)
                    if f is not None:
                        front(f, t, ch)
                    if a is not None and k < 8:
                        head_max(a, k, n)
                    if a is not None and n == 3 and k < 8:
                        max_rows(a, k)
                    if bg is not None:
                        back(bg, t, Y[1] if a is not None else M[1], chb, s_)
                    if s_ is not None and t == 4 * SLOTS_S - (1 if f is None else 0):
                        y_out(s_)
                    if f is not None and t == TAIL:
                        commit(f)
                        if is_first(f):
                            dve.tensor_copy(x2[:], x2n[:])
                    if nxt is not None and t - JOBS in (1, 3):
                        attend_split(nxt, (t - JOBS) // 2)
                if chb is not None:
                    chb.done()
                if ch is not None and part == 0:
                    assert ch.n == CSPLIT, ch.n
                if ch is not None and part == 1:
                    ch.done()

            def between(a, g, f):
                if is_first(a):
                    attend_split(a, 0)
                    attend_split(a, 1)
                if a is not None:
                    attend_v(a)
                if is_first(a):
                    prepare_rest()
                if g is not None and f is None:
                    ch = Chain(dve, c_back, g, CBACK)
                    for t in range(STEPS_B):
                        back(g, t, M[1], ch, None)
                    ch.done()

            def back(g, t, W, ch, f):
                if t == 1:
                    dve.wait_ge(b_pe, BPE * g + 1)
                    norm_stats(norms[1], tiles(W), ch, varb_ready)
                    if f is not None:
                        dve.tensor_copy(x2[:], x2n[:])
                top, total, prob, kmax, pos, first, kept, slot = (r4[:, n, :] for n in range(8))
                wide = lambda a: a.unsqueeze(2).to_broadcast([P, TT, EXPERTS])
                if t == 5:
                    dve.wait_ge(b_pe, BPE * g + 3)
                    ch.link(dve.tensor_copy(lg[:].rearrange("p t e -> p (t e)"), W[:, 0:TT * EXPERTS]))
                    ch.link(dve.tensor_reduce(top, lg[:], AX, ALU.max))
                    dve.tensor_tensor(lg[:], lg[:], wide(top), ALU.subtract).then_inc(b_dve, 1)
                if t == 7:
                    dve.wait_ge(b_dve, BDVE * g + 2)
                    ch.link(dve.scalar_tensor_tensor(oh[:], lg[:], 0.0, key8[:], ALU.is_ge, ALU.mult))
                    ch.link(dve.tensor_reduce(kmax, oh[:], AX, ALU.max))
                    dve.tensor_tensor(oh[:], key8[:], wide(kmax), ALU.is_equal).then_inc(b_dve, 1)
                if t == 8:
                    dve.wait_ge(b_act, BACT * g + 3)
                    ch.link(dve.tensor_reduce(total, lge[:], AX, ALU.add))
                    ch.link(dve.reciprocal(prob, total))
                    dve.tensor_scalar(first, kmax, -float(CAP), float(CAP * EXPERTS), ALU.mult, ALU.add)
                    dve.wait_ge(b_pe, BPE * g + 4)
                    ch.link(dve.tensor_tensor(lge[:], W[:, 0:TT * EXPERTS].rearrange("p (t e) -> p t e", t=TT),
                                              carry[:].unsqueeze(1).to_broadcast([P, TT, EXPERTS]), ALU.add))
                    ch.link(dve.tensor_tensor(lge[:], lge[:], oh[:], ALU.mult))
                    dve.tensor_tensor(carry[:], carry[:], W[:, 32:32 + EXPERTS], ALU.add)
                    ch.link(dve.tensor_reduce(pos, lge[:], AX, ALU.add))
                    ch.link(dve.tensor_scalar(kept, pos, float(CAP), None, ALU.is_le))
                    ch.link(dve.tensor_tensor(gate[:, bass.ds(g * TT, TT)], prob, kept, ALU.mult))
                    ch.link(dve.tensor_scalar(slot, pos, float(CAP), -1.0, ALU.min, ALU.add))
                    ch.link(dve.tensor_tensor(slot, slot, first, ALU.add))
                    dve.tensor_copy(x3[:, :, P], dump[:])
                    ch.link(dve.tensor_tensor(pos, slot, dump[:], ALU.subtract))
                    ch.link(dve.tensor_tensor(pos, pos, kept, ALU.mult))
                    ch.link(dve.tensor_tensor(pos, pos, dump[:], ALU.add))
                    ch.link(dve.tensor_scalar(dump[:], dump[:], float(T), None, ALU.add))
                    dve.tensor_copy(sidx[:], pos).then_inc(b_dve, 1)

            stages(dve, phase, between)

            ch = Chain(dve, c_exp, 0, 2 * EXPERTS)
            for e in range(EXPERTS):
                w = e % 2
                dve.wait_ge(tok_in[w], 16 * (e // 2 + 1))
                if e >= 2:
                    dve.wait_ge(rows_out[w], 16 * ST * (e // 2))
                ch.link(dve.scalar_tensor_tensor(mark[w][:], xe[w][:, :, P], 0.0, spare[:, e * ST:(e + 1) * ST],
                                                 ALU.is_equal, ALU.mult))
                ch.link(dve.scalar_tensor_tensor(mark[w][:], xe[w][:, :, P], -float(SLOTS), mark[w][:], ALU.add, ALU.add))
                dve.tensor_copy(eidx[w][:], mark[w][:]).then_inc(e_idx, 1)
                dve.wait_ge(we_in[w], 48 * (e // 2 + 1))
                dve.wait_ge(e_pe, down_count(e))
                dve.tensor_tensor(ye[w], Y[w][:, 0:CAP].rearrange("p (t c) -> p t c", c=P),
                                  b2s[w].unsqueeze(1).to_broadcast([P, ST, P]), ALU.add).then_inc(e_dve, 1)
            for g in range(GROUPS):
                ch = Chain(dve, c_back, 0, CBACK * GROUPS + 4 * (g + 1))
                ch.n = CBACK * GROUPS + 4 * g
                res = res4[g % 2]
                if g >= 2:
                    dve.wait_ge(z_act, g - 1)
                mine = x3all[:, g * TT:(g + 1) * TT, :]
                got = yall[:, g * TT:(g + 1) * TT, :]
                dve.wait_ge(y_loaded[g], 16)
                dve.wait_ge(b_act, BACT * GROUPS)
                ch.link(dve.tensor_tensor(got, got, gate[:, g * TT:(g + 1) * TT].unsqueeze(2)
                                          .to_broadcast([P, TT, P]), ALU.mult))
                ch.link(dve.tensor_tensor(res, got, mine, ALU.add))
                norm_stats(norms[g % 2], res, ch, varb_ready)
                ch.done()

        @block.gpsimd
        def _(pool):
            pool.memset(zeros[:], 0.0).then_inc(consts, 1)
            pool.memset(ident[:], 0.0).then_inc(consts, 1)
            pool.memset(ones[:], 1.0).then_inc(consts, 1)
            pool.memset(mhalf[:], -0.5).then_inc(consts, 1)
            pool.iota(key8i[:], pattern=[[0, TT], [-1, EXPERTS]], base=EXPERTS, channel_multiplier=0
                      ).then_inc(consts, 1)
            pool.iota(dumpi[:], pattern=[[P, TT]], base=SLOTS, channel_multiplier=1).then_inc(consts, 1)
            pool.iota(sparei[:], pattern=[[P, SLOTS // P]], base=SLOTS + N, channel_multiplier=1).then_inc(consts, 1)
            pool.wait_ge(consts, 7)
            pool.affine_select(out=ident[:], in_=ident[:], compare_op=ALU.not_equal, fill=1.0, base=0,
                               pattern=[[-1, P]], channel_multiplier=1).then_inc(consts, 1)
            pool.affine_select(out=tri[:], in_=ones[:], compare_op=ALU.is_ge, fill=0.0, base=0,
                               pattern=[[1, P]], channel_multiplier=-1).then_inc(consts, 1)
            assert CONSTS == 9

            def power(norm, ready, own, signal, count):
                vpe, negmean, rstd, shift = norm[2:]
                pool.wait_ge(ready, count)
                pool.tensor_tensor(rstd[:], vpe[:], mhalf[:], ALU.pow).then_inc(own, 1)
                pool.wait_ge(own, count)
                pool.tensor_tensor(shift[:], negmean[:], rstd[:], ALU.mult).then_inc(signal, 1)

            def increments(g, st, half):
                c, db, at = st // DB, st % DB, slice(2 * half, 2 * half + 2)
                if half == 0:
                    if st == 0:
                        pool.wait_ge(committed, g + 1)
                    pool.wait_ge(b_in[c % 2], 16 * (2 * g + c // 2 + 1))
                    if st == 2:
                        wait(pool, b_pe, BPE * (g - 1) + 1)
                    if st >= 3:
                        pool.wait_ge(y_mm, 8 * g + st - 2)
                pool.tensor_tensor(u[st % 3][:, at, :], brep[c % 2][:, at, :],
                                   dx[:, db, :].unsqueeze(1).to_broadcast([P, 2, T]), ALU.mult).then_inc(u_ready, 1)

            def forget(g, st):
                wait_apart(pool, da_ready, 8 * g + st + 1)
                pool.memset(da[st % 2][:].rearrange("p n (b t) -> p n b t", b=NB)[:, :, :, 0:1], 0.0
                            ).then_inc(u_ready, 1)

            def fold(g, st):
                pool.wait_ge(h_ready, 2 * (8 * g + st + 1))
                ub = u[st % 3]
                pool.tensor_tensor(ub[:, 0:2, :], ub[:, 0:2, :], ub[:, 2:4, :], ALU.add).then_inc(a_ready, 1)

            def front(g, t):
                if t == 3:
                    pool.wait_ge(x_in, 16 * (g + 1))
                    pool.tensor_tensor(xtok[:], xtok[:], bproj_row.unsqueeze(1).to_broadcast([P, TT, P]), ALU.add
                                       ).then_inc(f_pool, 1)
                if t == 9:
                    power(norms[0], varf_ready, powf, rstdf_ready, 2 * g + 1)
                if t == 12:
                    pool.wait_ge(f_act, FACT * g + 2)
                    pool.tensor_tensor(xtok[:], x1[:], bff_row.unsqueeze(1).to_broadcast([P, TT, P]), ALU.add
                                       ).then_inc(f_pool, 1)
                if t == 17:
                    power(norms[0], varf_ready, powf, rstdf_ready, 2 * g + 2)

            def scatter(g):
                wait_apart(pool, b_dve, BDVE * (g + 1))
                pool.wait_ge(zeroed, 16 * 2)
                for t in range(TT):
                    pool.indirect_dma_start(buf, bass.IndirectOffsetOnAxis(ap=sidx[:, t:t + 1], axis=0),
                                            x3[:, t, :], None).then_inc(scattered, 16)

            def phase(part, a, f, s_, nxt=None):
                bg = back_of(s_) if part == 0 else None
                if s_ is not None and part == 0:
                    increments(s_, 0, 0)
                    forget(s_, 0)
                    increments(s_, 0, 1)
                for t, k, n in subslots(part, a, f, s_):
                    if f is not None:
                        front(f, t)
                    if bg is not None and t == 2:
                        power(norms[1], varb_ready, powb, rstdb_ready, bg + 1)
                    if s_ is not None:
                        if n == 0 and 1 <= k <= 8 and a is not None:
                            fold(s_, k - 1)
                        if n in (1, 2) and k < 7:
                            increments(s_, k + 1, n - 1)
                        if n == 3 and k < 7:
                            forget(s_, k + 1)
                    if bg is not None and t == 9:
                        scatter(bg)
                    if bg is not None and t == SPLIT - 1:
                        pool.wait_ge(scattered, 16 * TT * (bg + 1))

            def between(a, g, f):
                if g is not None and f is None:
                    power(norms[1], varb_ready, powb, rstdb_ready, g + 1)
                    scatter(g)

            pool.wait_ge(w_in, 16 * LOADS)
            stages(pool, phase, between)

            for e in range(EXPERTS):
                w = e % 2
                pool.wait_ge(e_dve, e + 1)
                pool.wait_ge(e_idx, e + 1)
                for t in range(ST):
                    pool.indirect_dma_start(y, bass.IndirectOffsetOnAxis(ap=eidx[w][:, t:t + 1], axis=0),
                                            ye[w][:, t, :], None).then_inc(rows_out[w], 16)
            for g in range(GROUPS):
                power(norms[g % 2], varb_ready, powb, rstdb_ready, GROUPS + g + 1)


def kernel(**inputs):
    import numpy as np
    import concourse.bacc as bacc
    from concourse.bass_utils import run_bass_kernel_spmd as run

    a = {k: np.asarray(v) for k, v in inputs.items()}
    x = a["L0_attn_x"]
    B, S, C = x.shape
    flat = x.reshape(B * S, C)
    by_block = lambda v: v.reshape(DB, P, -1).transpose(1, 0, 2).reshape(P, -1)
    bq = a["L0_attn_b_qkv"]
    arrays = {
        "xT": flat.T, "x": flat,
        "wqkv": a["L0_attn_W_qkv"], "abqkv": np.concatenate([a["L0_attn_A_qkv"].T, a["L0_attn_B_qkv"]], 1),
        "wproj": a["L0_attn_W_proj"], "abproj": np.concatenate([a["L0_attn_A_proj"].T, a["L0_attn_B_proj"]], 1),
        "rows": np.concatenate([bq[2 * C:], a["L0_attn_b_proj"], a["L0_ffn_bias"], a["L1_attn_w_dt"]]),
        "cols": np.concatenate([bq[0:C, None], bq[C:2 * C, None], by_block(a["L1_attn_conv_w"]),
                                by_block(a["L1_attn_conv_b"]), by_block(a["L1_attn_D_param"]),
                                by_block(a["L1_attn_b_dt"]), by_block(a["L1_attn_A_log"])], 1),
        "wfp8T": a["L0_ffn_weight_fp8"].T,
        "scales": np.concatenate([a["L0_ffn_input_scale"], a["L0_ffn_weight_scale"]]),
        "win": a["L1_attn_W_in"], "wx": a["L1_attn_W_xproj"], "wout": a["L1_attn_W_out"],
        "rwT": a["L1_ffn_router_w"].T, "w1": a["L1_ffn_w1"],
        "b1c": a["L1_ffn_b1"].reshape(EXPERTS, FB, P).transpose(2, 0, 1),
        "w2": a["L1_ffn_w2"], "b2": a["L1_ffn_b2"],
    }
    arrays = {"in_" + k: np.ascontiguousarray(v) for k, v in arrays.items()}
    nc = bacc.Bacc("TRN2", target_bir_lowering=False, num_devices=1)
    args = [nc.dram_tensor(k, v.shape, F32, kind="ExternalInput").ap() for k, v in arrays.items()]
    N = B * S
    slots = EXPERTS * -(-3 * N // (2 * EXPERTS))
    buf = nc.dram_tensor("slots", (slots + N, C + 1), F32, kind="Internal").ap()
    y = nc.dram_tensor("expert_rows", (N + slots, C), F32, kind="Internal").ap()
    parts = [nc.dram_tensor(f"parts{n}", (HEADS, len(QPARTS), HD, T), BF16, kind="Internal").ap() for n in range(2)]
    bcd = nc.dram_tensor("b_and_c", (N // T, 2 * STATES, T), F32, kind="Internal").ap()
    out = nc.dram_tensor("out_0", (N, C), F32, kind="ExternalOutput").ap()
    layers(nc, *args, buf, y, parts, bcd, out)
    r = run(nc, [arrays], core_ids=[0])
    return r.results[0]["out_0"].reshape(B, S, C)
```
